# Optimizing a Trainium2 kernel written in Bass

```python
import numpy as np
import jax
import jax.numpy as jnp

def _softmax(x, axis=-1):
    return jax.nn.softmax(x, axis=axis)

def _gelu(x):
    return jax.nn.gelu(x, approximate=True)

def _silu(x):
    return jax.nn.silu(x)

def _sigmoid(x):
    return jax.nn.sigmoid(x)

def _layernorm(x, axis=-1, eps=1e-05):
    m = jnp.mean(x, axis=axis, keepdims=True)
    v = jnp.var(x, axis=axis, keepdims=True)
    return (x - m) / jnp.sqrt(v + eps)

def _scatter_add(tgt, idx, src, axis=0):
    return tgt.at[idx].add(src)

def _segment_sum(src, seg, n):
    return jax.ops.segment_sum(src, seg, n)
kernel_name = 'mk_xattn_ffn_d2_seqx_r8_b34d01'

def setup_inputs(seed: int=0):
    np.random.seed(seed)
    _w = jnp.asarray

    def _rec_inputs():
        import jax
        import jax.numpy as jnp
        _rk = jax.random.key(seed)
        x = -0.0001033 + 0.9999 * jax.random.normal(jax.random.fold_in(_rk, 1), (2, 512, 128), jnp.float32)
        _lenS = 512 - jax.random.randint(jax.random.fold_in(_rk, 7), (2,), 0, max(1, 512 // 4) + 1, jnp.int32)
        _lenS2 = 77 - jax.random.randint(jax.random.fold_in(_rk, 8), (2,), 0, max(1, 77 // 4) + 1, jnp.int32)
        _ctx_1024P = jax.random.normal(jax.random.fold_in(_rk, 11), (2, 16, 128), jnp.float32)
        _ctx_1024c = jax.random.dirichlet(jax.random.fold_in(_rk, 511), 0.3 * jnp.ones((16,), jnp.float32), (2, 77))
        _ctx_1024t = jnp.einsum('bsk,bkd->bsd', _ctx_1024c, _ctx_1024P)
        _ctx_1024t = _ctx_1024t * jax.lax.rsqrt(jnp.mean(jnp.square(_ctx_1024t)) + 1e-12) * 0.953939
        ctx_1024 = -0.000292821 + 1.00034 * (_ctx_1024t + 0.3 * jax.random.normal(jax.random.fold_in(_rk, 611), (2, 77, 128), jnp.float32))
        return (x, ctx_1024)
    x, ctx_1024 = _rec_inputs()

    def _L0_xattn_setup():
        import jax, jax.numpy as jnp
        import numpy as np
        from jax import lax
        B, T, F = (32, 128, 128)
        CONV_UNITS = 256
        SHORT_UNITS = 256
        RATE = 4
        key = jax.random.key(seed)
        k1, k2, k3 = jax.random.split(key, 3)
        inputs = jax.random.normal(k1, (B, T, F), dtype=jnp.float32)
        memory = jax.random.normal(k2, (B, CONV_UNITS + SHORT_UNITS, F), dtype=jnp.float32)
        conv_w = jax.random.normal(k3, (RATE, F, F), dtype=jnp.float32) * 0.02
        conv_b = jnp.zeros((F,), dtype=jnp.float32)
        return {'inputs': inputs, 'memory': memory, 'conv_w': conv_w, 'conv_b': conv_b, 'conv_units': CONV_UNITS, 'short_units': SHORT_UNITS, 'rate': RATE}
    _L0_xattn_all = _L0_xattn_setup()
    _L0_xattn_in = {k: v for k, v in _L0_xattn_all.items() if k in ('conv_w', 'conv_b')}
    del _L0_xattn_all

    def _L0_ffn_setup():
        import jax, jax.numpy as jnp
        import numpy as np
        B, T = (2, 256)
        D_MODEL, D_HIDDEN = (128, 256)
        N_EXPERTS, TOP_K = (8, 2)
        N_TOKENS = B * T
        CAPACITY = 2 * N_TOKENS * TOP_K // N_EXPERTS
        key = jax.random.key(seed)
        k_x, k_rw, k_w, k_v, k_o = jax.random.split(key, 5)
        x = jax.random.normal(k_x, (B, T, D_MODEL), jnp.float32)
        router_w = jax.random.normal(k_rw, (N_EXPERTS, D_MODEL), jnp.float32) * D_MODEL ** (-0.5)
        router_b = jnp.zeros((N_EXPERTS,), jnp.float32)
        W = jax.random.normal(k_w, (N_EXPERTS, D_MODEL, D_HIDDEN), jnp.float32) * D_MODEL ** (-0.5)
        V = jax.random.normal(k_v, (N_EXPERTS, D_MODEL, D_HIDDEN), jnp.float32) * D_MODEL ** (-0.5)
        W_out = jax.random.normal(k_o, (N_EXPERTS, D_HIDDEN, D_MODEL), jnp.float32) * D_HIDDEN ** (-0.5)
        return {'x': x, 'router_w': router_w, 'router_b': router_b, 'W': W, 'V': V, 'W_out': W_out}
    _L0_ffn_all = _L0_ffn_setup()
    _L0_ffn_in = {k: v for k, v in _L0_ffn_all.items() if k in ('router_w', 'router_b', 'W', 'V', 'W_out')}
    del _L0_ffn_all

    def _L1_xattn_setup():
        import jax, jax.numpy as jnp
        import numpy as np
        DIM = 128
        NUM_HEADS = 16
        HEAD_DIM = DIM // NUM_HEADS
        key = jax.random.key(seed)
        ks = jax.random.split(key, 11)
        B, N, C = (2, 256, DIM)
        s = 1.0 / np.sqrt(C)
        inp = {'q': jax.random.normal(ks[0], (B, N, C), jnp.float32), 'k': jax.random.normal(ks[1], (B, N, C), jnp.float32), 'v': jax.random.normal(ks[2], (B, N, C), jnp.float32), 'Wq': jax.random.normal(ks[3], (C, C), jnp.float32) * s, 'bq': jnp.zeros((C,), jnp.float32), 'Wk': jax.random.normal(ks[4], (C, C), jnp.float32) * s, 'bk': jnp.zeros((C,), jnp.float32), 'Wv': jax.random.normal(ks[5], (C, C), jnp.float32) * s, 'bv': jnp.zeros((C,), jnp.float32), 'Wo': jax.random.normal(ks[6], (C, C), jnp.float32) * s, 'bo': jnp.zeros((C,), jnp.float32)}
        return inp
    _L1_xattn_all = _L1_xattn_setup()
    _L1_xattn_in = {k: v for k, v in _L1_xattn_all.items() if k in ('Wq', 'bq', 'Wk', 'bk', 'Wv', 'bv', 'Wo', 'bo')}
    del _L1_xattn_all

    def _L1_ffn_setup():
        import jax, jax.numpy as jnp
        import numpy as np
        NUM_EXPERTS = 160
        TOP_K = 8
        ROUTED_SCALE = 2.5
        HIDDEN = 128
        INTER = 64
        key = jax.random.key(seed)
        ks = jax.random.split(key, 7)
        B, S = (1, 256)
        return {'hidden_states': jax.random.normal(ks[0], (B, S, HIDDEN), dtype=jnp.float32), 'router_w': jax.random.normal(ks[1], (NUM_EXPERTS, HIDDEN), dtype=jnp.float32) * 0.02, 'expert_bias': jnp.zeros((NUM_EXPERTS,), dtype=jnp.float32), 'w_gate': jax.random.normal(ks[2], (NUM_EXPERTS, INTER, HIDDEN), dtype=jnp.float32) * 0.02, 'w_down': jax.random.normal(ks[3], (NUM_EXPERTS, HIDDEN, INTER), dtype=jnp.float32) * 0.02, 'w_gate_shared': jax.random.normal(ks[4], (INTER, HIDDEN), dtype=jnp.float32) * 0.02, 'w_down_shared': jax.random.normal(ks[5], (HIDDEN, INTER), dtype=jnp.float32) * 0.02}
    _L1_ffn_all = _L1_ffn_setup()
    _L1_ffn_in = {k: v for k, v in _L1_ffn_all.items() if k in ('router_w', 'expert_bias', 'w_gate', 'w_down', 'w_gate_shared', 'w_down_shared')}
    del _L1_ffn_all
    return {'x': x, 'ctx_1024': ctx_1024, 'L0_xattn_conv_w': _L0_xattn_in['conv_w'], 'L0_xattn_conv_b': _L0_xattn_in['conv_b'], 'L0_ffn_router_w': _L0_ffn_in['router_w'], 'L0_ffn_router_b': _L0_ffn_in['router_b'], 'L0_ffn_W': _L0_ffn_in['W'], 'L0_ffn_V': _L0_ffn_in['V'], 'L0_ffn_W_out': _L0_ffn_in['W_out'], 'L1_xattn_Wq': _L1_xattn_in['Wq'], 'L1_xattn_bq': _L1_xattn_in['bq'], 'L1_xattn_Wk': _L1_xattn_in['Wk'], 'L1_xattn_bk': _L1_xattn_in['bk'], 'L1_xattn_Wv': _L1_xattn_in['Wv'], 'L1_xattn_bv': _L1_xattn_in['bv'], 'L1_xattn_Wo': _L1_xattn_in['Wo'], 'L1_xattn_bo': _L1_xattn_in['bo'], 'L1_ffn_router_w': _L1_ffn_in['router_w'], 'L1_ffn_expert_bias': _L1_ffn_in['expert_bias'], 'L1_ffn_w_gate': _L1_ffn_in['w_gate'], 'L1_ffn_w_down': _L1_ffn_in['w_down'], 'L1_ffn_w_gate_shared': _L1_ffn_in['w_gate_shared'], 'L1_ffn_w_down_shared': _L1_ffn_in['w_down_shared']}

def reference(x, ctx_1024, L0_xattn_conv_w, L0_xattn_conv_b, L0_ffn_router_w, L0_ffn_router_b, L0_ffn_W, L0_ffn_V, L0_ffn_W_out, L1_xattn_Wq, L1_xattn_bq, L1_xattn_Wk, L1_xattn_bk, L1_xattn_Wv, L1_xattn_bv, L1_xattn_Wo, L1_xattn_bo, L1_ffn_router_w, L1_ffn_expert_bias, L1_ffn_w_gate, L1_ffn_w_down, L1_ffn_w_gate_shared, L1_ffn_w_down_shared):
    import jax
    import jax.numpy as jnp

    def _L0_xattn_ref(inputs, memory, conv_w, conv_b, conv_units, short_units, rate):
        import jax, jax.numpy as jnp
        import numpy as np
        from jax import lax
        B, T, F = (32, 128, 128)
        CONV_UNITS = 256
        SHORT_UNITS = 256
        RATE = 4
        b, t, f = inputs.shape
        conv_mem = memory[:, :conv_units]
        short_mem = memory[:, -short_units:]
        old_memory = short_mem[:, :t]
        compression = lax.conv_general_dilated(old_memory, conv_w, window_strides=(rate,), padding='VALID', dimension_numbers=('NWC', 'WIO', 'NWC')) + conv_b
        tc = compression.shape[1]
        new_short = jnp.concatenate([short_mem[:, t:], inputs], axis=1)
        new_conv = jnp.concatenate([conv_mem[:, tc:], compression], axis=1)
        return jnp.concatenate([new_conv, new_short], axis=1)

    def _L0_ffn_ref(x, router_w, router_b, W, V, W_out):
        import jax, jax.numpy as jnp
        import numpy as np
        B, T = (2, 256)
        D_MODEL, D_HIDDEN = (128, 256)
        N_EXPERTS, TOP_K = (8, 2)
        N_TOKENS = B * T
        CAPACITY = 2 * N_TOKENS * TOP_K // N_EXPERTS
        Bq, Tq, D = x.shape
        N = Bq * Tq
        x_flat = x.reshape(N, D)
        router_logits = x_flat @ router_w.T + router_b
        top_vals, top_ids = jax.lax.top_k(router_logits, TOP_K)
        top_probs = jax.nn.softmax(top_vals, axis=-1)
        x_pad = jnp.concatenate([x_flat, jnp.zeros((1, D), x_flat.dtype)], axis=0)
        probs_pad = jnp.concatenate([top_probs, jnp.zeros((1, TOP_K), top_probs.dtype)], axis=0)
        out = jnp.zeros((N + 1, D), x_flat.dtype)
        for e in range(N_EXPERTS):
            tok, slot = jnp.nonzero(top_ids == e, size=CAPACITY, fill_value=(N, 0))
            w = probs_pad[tok, slot][:, None]
            xin = x_pad[tok]
            a = xin @ W[e]
            b = xin @ V[e]
            y = a * (b * jax.nn.sigmoid(b)) @ W_out[e]
            out = out.at[tok].add(y * w)
        return out[:N].reshape(Bq, Tq, D)

    def _L1_xattn_ref(q, k, v, Wq, bq, Wk, bk, Wv, bv, Wo, bo):
        import jax, jax.numpy as jnp
        import numpy as np
        DIM = 128
        NUM_HEADS = 16
        HEAD_DIM = DIM // NUM_HEADS
        B, Nq, C = q.shape
        Nkv = k.shape[1]
        H, D = (NUM_HEADS, HEAD_DIM)
        qh = (q @ Wq.T + bq).reshape(B, Nq, H, D).transpose(0, 2, 1, 3)
        kh = (k @ Wk.T + bk).reshape(B, Nkv, H, D).transpose(0, 2, 1, 3)
        vh = (v @ Wv.T + bv).reshape(B, Nkv, H, D).transpose(0, 2, 1, 3)
        scale = D ** (-0.5)
        attn = jax.nn.softmax(jnp.einsum('bhqd,bhkd->bhqk', qh, kh) * scale, axis=-1)
        out = jnp.einsum('bhqk,bhkd->bhqd', attn, vh)
        out = out.transpose(0, 2, 1, 3).reshape(B, Nq, C)
        return out @ Wo.T + bo

    def _L1_ffn_ref(hidden_states, router_w, expert_bias, w_gate, w_down, w_gate_shared, w_down_shared):
        import jax, jax.numpy as jnp
        import numpy as np
        NUM_EXPERTS = 160
        TOP_K = 8
        ROUTED_SCALE = 2.5
        HIDDEN = 128
        INTER = 64
        B, S, H = hidden_states.shape
        x = hidden_states.reshape(-1, H)
        T = x.shape[0]
        logits = x @ router_w.T + expert_bias[None, :]
        probs = jax.nn.sigmoid(logits)
        top_w, top_idx = jax.lax.top_k(probs, TOP_K)
        top_w = top_w / (jnp.sum(top_w, axis=-1, keepdims=True) + 1e-09)
        top_w = top_w * ROUTED_SCALE
        combine = jnp.zeros((T, NUM_EXPERTS), dtype=x.dtype)
        combine = combine.at[jnp.arange(T)[:, None], top_idx].set(top_w)
        h1 = jax.nn.silu(jnp.einsum('th,eih->eti', x, w_gate))
        h1w = h1 * combine.T[:, :, None]
        routed = jnp.einsum('eti,ehi->th', h1w, w_down)
        shared = jax.nn.silu(x @ w_gate_shared.T) @ w_down_shared.T
        return (routed + shared).reshape(B, S, H)
    x = x + _L0_xattn_ref(ctx_1024, _layernorm(x, axis=-1), L0_xattn_conv_w, L0_xattn_conv_b, 256, 256, 4)
    x = x + _L0_ffn_ref(_layernorm(x, axis=-1), L0_ffn_router_w, L0_ffn_router_b, L0_ffn_W, L0_ffn_V, L0_ffn_W_out)
    x = x + _L1_xattn_ref(_layernorm(x, axis=-1), ctx_1024, ctx_1024, L1_xattn_Wq, L1_xattn_bq, L1_xattn_Wk, L1_xattn_bk, L1_xattn_Wv, L1_xattn_bv, L1_xattn_Wo, L1_xattn_bo)
    x = x + _L1_ffn_ref(_layernorm(x, axis=-1), L1_ffn_router_w, L1_ffn_expert_bias, L1_ffn_w_gate, L1_ffn_w_down, L1_ffn_w_gate_shared, L1_ffn_w_down_shared)
    return x

_drawn_inputs = setup_inputs


def setup_inputs(seed=0):
    import zlib

    import numpy as np

    out = dict(_drawn_inputs(seed))
    spreads = {'L0_xattn_conv_b': (0.0, 0.423),
     'L0_ffn_router_b': (0.0, 0.1),
     'L1_xattn_bq': (0.0, 0.473),
     'L1_xattn_bk': (0.0, 0.8),
     'L1_xattn_bv': (0.0, 0.1),
     'L1_xattn_bo': (0.0, 0.1),
     'L1_ffn_expert_bias': (0.0, 0.8)}
    factors = {'L1_ffn_router_w': 5.717,
     'L1_ffn_w_gate': 5.446,
     'L1_ffn_w_down': 5.412,
     'L1_ffn_w_gate_shared': 4.811,
     'L1_ffn_w_down_shared': 4.705}
    for name, (base, spread) in spreads.items():
        noise = np.random.default_rng([zlib.crc32(name.encode()), seed]).standard_normal(out[name].shape)
        drawn = base * np.exp(spread * noise) if base else spread * noise
        out[name] = jnp.asarray(drawn.astype(out[name].dtype))
    for name, factor in factors.items():
        out[name] = (out[name] * factor).astype(out[name].dtype)
    return out
```

```python
import concourse.bass as bass
from concourse import mybir
from contextlib import ExitStack

F32 = mybir.dt.float32
F32R = mybir.dt.float32r
BF16 = mybir.dt.bfloat16
ALU = mybir.AluOpType
ACT = mybir.ActivationFunctionType
AX = mybir.AxisListType

P = 128
B, T, C = 2, 512, 77
NT = B * T // P
HALF = 512
EPS = 1e-5
UNITS, RATE = 256, 4
NCONV = (C - RATE) // RATE + 1
CONV_ROWS = NCONV * RATE
E0, HID0, CAPACITY = 8, 256, 256
H, D = 16, 8
GROUPS, HG = 4, 4
STACK = 3 * HG * D
SCALE = D ** -0.5
E1, INTER, TOP, ROUTED_SCALE = 160, 64, 8, 2.5
KT = 4
EK = E1 // KT
ROUNDS1 = EK // 2
SIG_LOW, SIG_HIGH = -88.72, 17.33

SPLIT = {}
_at = 0
for _name, _n in (("rw0", E0), ("ctxT", B * C), ("wk", GROUPS * STACK), ("wv", P), ("wq", GROUPS * STACK),
                  ("wo", P), ("rw1", E1), ("wgs", P), ("wds", P)):
    SPLIT[_name] = (_at, _at + _n)
    _at += _n
NSPLIT = _at
IDENT, ULT, ONES, TRI, HMASK, HSEL = 0, P, 2 * P, 3 * P, 3 * P + 64, 3 * P + 68
NCONST = 3 * P + 84
RB0, BV, BO, EB = 0, E0, E0 + P, E0 + 2 * P
NROWS = E0 + 2 * P + E1


def build_program(nc, x, ctx, conv_w, conv_b, split_in, consts_in, rows_in, bqk_in, w0_in, sel0_in, w1_in, sel1_in, out):
    stack = ExitStack()
    with stack:
        def sb(name, shape, dt=F32):
            return stack.enter_context(nc.sbuf_tensor(name, shape, dt))

        def sem(name):
            return stack.enter_context(nc.semaphore(name))

        resid = sb("resid", [P, NT, P])
        shifted = sb("shifted", [P, NT + B, P])
        addend = sb("addend", [P, NT, P])
        xn = sb("xn", [P, NT + B, P])
        stats = sb("stats", [P, NT + B, 6])
        mv = sb("mv", [P, NT + B, 2])
        std = sb("std", [P, NT + B, 1])
        rstd = sb("rstd", [P, NT + B, 1])
        xT_hi = sb("xT_hi", [P, NT * P], F32R)
        xT_lo = sb("xT_lo", [P, NT * P], F32R)
        conv_w_sb = sb("conv_w_sb", [P, RATE, P])
        conv_x = sb("conv_x", [P, B, RATE, P])
        par = sb("par", [P, NSPLIT])
        par_hi = sb("par_hi", [P, NSPLIT], F32R)
        par_lo = sb("par_lo", [P, NSPLIT], F32R)
        const = sb("const", [P, NCONST])
        ident_bf = sb("ident_bf", [P, P], BF16)
        rows = sb("rows", [P, NROWS])
        bqk = sb("bqk", [STACK, 2 * GROUPS])
        eps = sb("eps", [P, 1])
        lg0 = sb("lg0", [P, NT, E0])
        pair_gt = sb("pair_gt", [P, NT, E0, E0])
        pair_eq = sb("pair_eq", [P, NT, E0, E0])
        rank0 = sb("rank0", [P, NT, E0])
        first0 = sb("first0", [P, NT, E0])
        second0 = sb("second0", [P, NT, E0])
        chosen0 = sb("chosen0", [P, NT, E0])
        comb0 = sb("comb0", [P, NT, E0])
        tmp0 = sb("tmp0", [P, NT, E0])
        top0 = sb("top0", [P, 6, NT])
        parts0 = sb("parts0", [P, NT, 3, E0], BF16)
        combT0 = sb("combT0", [3 * E0, NT * P], BF16)
        lg1 = sb("lg1", [P, NT, E1])
        key1 = sb("key1", [P, NT, E1])
        prob1 = sb("prob1", [P, NT, E1])
        comb1 = sb("comb1", [P, NT, E1])
        best1 = sb("best1", [P, NT, TOP])
        sum1 = sb("sum1", [P, NT])
        parts1 = sb("parts1", [P, NT, KT, 3, EK], BF16)
        combT1 = sb("combT1", [3 * EK, KT, NT * P], BF16)
        k3 = sb("k3", [STACK, GROUPS, B, C])
        k3_part = sb("k3_part", [STACK, GROUPS, B, C], F32R)
        k_stack = sb("k_stack", [P, B, H, C], F32R)
        v_ones = sb("v_ones", [C, B, H, D + 1])
        q_stack = sb("q_stack", [P, GROUPS, NT * P], F32R)
        nmax = sb("nmax", [P, 2, H])
        nmax_pad = sb("nmax_pad", [P, 2, P])
        NE = 4
        exps = sb("exps", [C, NE, HALF])
        inv = sb("inv", [P, NT, H])
        onat = sb("onat", [P, NT, P])
        oT_hi = sb("oT_hi", [P, NT * P], F32R)
        oT_lo = sb("oT_lo", [P, NT * P], F32R)
        raw = [sb(f"raw{s}", [P, 1024]) for s in range(2)]
        w_hi = [sb(f"w_hi{s}", [P, 1024], F32R) for s in range(2)]
        w_lo = [sb(f"w_lo{s}", [P, 1024], F32R) for s in range(2)]
        sel = [sb(f"sel{s}", [3 * EK, P], BF16) for s in range(2)]
        silu_out = sb("silu_out", [P, 2, HALF])
        gated = sb("gated", [P, 2, HALF])
        hw = sb("hw", [P, 2, HALF])
        NH = 4
        h_hi = [sb(f"h_hi{i}", [P, HALF], F32R) for i in range(NH)]
        h_lo = [sb(f"h_lo{i}", [P, HALF], F32R) for i in range(NH)]
        yT = shifted[:, 0:NT, :].rearrange("p n d -> p (n d)")

        bank = [stack.enter_context(nc.psum_tensor(f"bank{i}", [P, HALF], F32)) for i in range(8)]
        acc = bank[6:8]

        def hi(name, a=0, b=None):
            s, e = SPLIT[name]
            return par_hi[:, s + a:(e if b is None else s + b)]

        def lo(name, a=0, b=None):
            s, e = SPLIT[name]
            return par_lo[:, s + a:(e if b is None else s + b)]

        ident = const[:, IDENT:IDENT + P]

        zeroed = sem("zeroed")
        x_loaded = sem("x_loaded")
        shift_loaded = sem("shift_loaded")
        add_loaded = sem("add_loaded")
        conv_loaded = sem("conv_loaded")
        par_loaded = sem("par_loaded")
        const_loaded = sem("const_loaded")
        rows_loaded = sem("rows_loaded")
        eps_set = sem("eps_set")
        par_split = sem("par_split")
        ident_cast = sem("ident_cast")
        dve_step = sem("dve_step")
        act_step = sem("act_step")
        pool_step = sem("pool_step")
        var_ready = sem("var_ready")
        std_ready = sem("std_ready")
        xn_ready = sem("xn_ready")
        xT_psum = sem("xT_psum")
        xT_hi_ready = sem("xT_hi_ready")
        xT_lo_ready = sem("xT_lo_ready")
        convT_psum = sem("convT_psum")
        conv_x_ready = sem("conv_x_ready")
        conv_done = sem("conv_done")
        logits0 = sem("logits0")
        diff_ready = sem("diff_ready")
        exp_ready = sem("exp_ready")
        chosen_ready = sem("chosen_ready")
        place_ready = sem("place_ready")
        parts0_ready = sem("parts0_ready")
        combT0_psum = sem("combT0_psum")
        combT0_ready = sem("combT0_ready")
        k_psum = sem("k_psum")
        v_psum = sem("v_psum")
        k3_ready = sem("k3_ready")
        k_stack_ready = sem("k_stack_ready")
        v_ready = sem("v_ready")
        q_psum = sem("q_psum")
        q_hi_ready = sem("q_hi_ready")
        q_lo_ready = sem("q_lo_ready")
        scores_ready = sem("scores_ready")
        nmax_ready = sem("nmax_ready")
        nmaxT_psum = sem("nmaxT_psum")
        q_max_ready = [sem(f"q_max_ready{b}") for b in range(B)]
        scoresT_ready = sem("scoresT_ready")
        exp_done = sem("exp_done")
        pv_done = sem("pv_done")
        onat_ready = sem("onat_ready")
        oT_psum = sem("oT_psum")
        oT_hi_ready = sem("oT_hi_ready")
        oT_lo_ready = sem("oT_lo_ready")
        proj_done = sem("proj_done")
        logits1 = sem("logits1")
        lg1_ready = sem("lg1_ready")
        prob_ready = sem("prob_ready")
        parts1_ready = sem("parts1_ready")
        combT1_psum = sem("combT1_psum")
        combT1_ready = sem("combT1_ready")
        shared_gate = sem("shared_gate")
        shared_silu = sem("shared_silu")
        shared_hi = sem("shared_hi")
        shared_lo = sem("shared_lo")
        shared_down = sem("shared_down")
        yT_ready = sem("yT_ready")
        y_psum = sem("y_psum")
        out_ready = sem("out_ready")
        stored = sem("stored")

        class Stream:

            def __init__(self, tag, rounds, per, two_gates, lag):
                self.rounds, self.per, self.two_gates, self.lag = rounds, per, two_gates, lag
                self.units = rounds * per
                self.loaded = [sem(f"{tag}_loaded{s}") for s in range(2)]
                self.split = sem(f"{tag}_split")
                self.b_ready = sem(f"{tag}_b_ready")
                self.a_ready = sem(f"{tag}_a_ready")
                self.c_ready = sem(f"{tag}_c_ready")
                self.silu = sem(f"{tag}_silu")
                self.gated = sem(f"{tag}_gated")
                self.hw = sem(f"{tag}_hw")
                self.hi = sem(f"{tag}_hi")
                self.lo = sem(f"{tag}_lo")
                self.down = sem(f"{tag}_down")

        s0 = Stream("l0", E0, 2 * (HID0 // P), True, 2)
        s1 = Stream("l1", ROUNDS1, 2 * KT, False, 3)

        def operands(s, v, slot):
            part, half = divmod(v, 2)
            cols = slice(half * HALF, (half + 1) * HALF)
            if s is s0:
                lin = slice(part * P, part * P + P)
                gate = slice(HID0 + part * P, HID0 + part * P + P)
                down = slice(2 * HID0 + part * P, 2 * HID0 + part * P + P)
                return gate, lin, down, sel[slot][0:3 * E0, :], combT0[:, cols], half
            gate = slice(part * P, part * P + P)
            down = slice(KT * P + part * P, KT * P + part * P + P)
            return gate, None, down, sel[slot][:, :], combT1[:, part, cols], half

        def wait(eng, s, value):
            if not (isinstance(value, int) and value <= 0):
                eng.wait_ge(s, value)

        def run_pairs(eng, s, body):
            body(0, 0)
            with eng.Fori(1, s.rounds // 2) as j:
                body(j * (2 * s.per), j * 2)

        block = stack.enter_context(nc.Block())

        @block.sync
        def _(sp):
            x_flat = x.rearrange("b t d -> (b t) d")
            sp.wait_ge(zeroed, 1)
            for b in range(B):
                t0 = b * (NT // B)
                last = UNITS - NCONV - P
                first = T - UNITS - C - P
                for dst, src in ((shifted[:, t0, :], x[b, NCONV:NCONV + P, :]),
                                 (shifted[0:last, t0 + 1, :], x[b, NCONV + P:UNITS, :]),
                                 (shifted[:, t0 + 2, :], x[b, UNITS + C:UNITS + C + P, :]),
                                 (shifted[0:first, t0 + 3, :], x[b, UNITS + C + P:T, :]),
                                 (shifted[0:CONV_ROWS, NT + b, :], x[b, UNITS:UNITS + CONV_ROWS, :])):
                    sp.dma_start(dst, src).then_inc(shift_loaded, 16)
            sp.dma_start(resid[:, :, :], x_flat.rearrange("(n p) d -> p n d", p=P)).then_inc(x_loaded, 16)

            def load(s, src, sel_src, cols, n_sel):
                def body(u, r):
                    for i in range(2):
                        if not isinstance(r, int) or r + i >= 2:
                            wait(sp, s.split, (r + i) * 2 - 2)
                            wait(sp, s.c_ready, u + (i - 1) * s.per)
                        elif s is s1:
                            sp.wait_ge(s0.c_ready, s0.units)
                            sp.wait_ge(s0.split, 2 * s0.rounds)
                        sp.dma_start(raw[i][:, 0:cols], src[r + i, :, :]).then_inc(s.loaded[i], 16)
                        sp.dma_start(sel[i][0:n_sel, :], sel_src[r + i, :, :]).then_inc(s.loaded[i], 16)
                run_pairs(sp, s, body)

            load(s0, w0_in, sel0_in.bitcast(BF16), 3 * HID0, 3 * E0)
            load(s1, w1_in, sel1_in.bitcast(BF16), 2 * KT * P, 3 * EK)
            for half in range(2):
                sp.wait_ge(out_ready, half + 1)
                n = NT // 2
                sp.dma_start(out.rearrange("b t d -> (b t) d").rearrange("(n p) d -> p n d", p=P)[:, half * n:half * n + n, :],
                             resid[:, half * n:half * n + n, :]).then_inc(stored, 16)
            sp.wait_ge(stored, 32)

        @block.gpsimd
        def _(pool):
            steps = [0]

            def step(ins):
                steps[0] += 1
                ins.then_inc(pool_step, 1)
                pool.wait_ge(pool_step, steps[0])

            pool.memset(shifted[:, :, :], 0.0).then_inc(zeroed, 1)
            pool.memset(addend[:, :, :], 0.0).then_inc(zeroed, 1)
            pool.memset(eps[:, :], EPS).then_inc(eps_set, 1)
            pool.memset(conv_x[:, :, :, :], 0.0).then_inc(zeroed, 1)
            pool.memset(nmax_pad[:, :, :], 0.0).then_inc(zeroed, 1)
            pool.memset(v_ones[:, :, :, :], 1.0).then_inc(zeroed, 1)
            pool.wait_ge(const_loaded, 16)
            pool.tensor_copy(ident_bf[:, :], ident).then_inc(ident_cast, 1)
            pool.wait_ge(par_loaded, 16)
            pool.tensor_copy(par_hi[:, :], par[:, :]).then_inc(par_split, 1)
            pool.wait_ge(par_split, 1)
            pool.tensor_tensor(par_lo[:, :], par[:, :], par_hi[:, :].bitcast(F32), ALU.subtract).then_inc(par_split, 1)

            def split(s, cols):
                def body(u, r):
                    for i in range(2):
                        pool.wait_ge(s.loaded[i], r * 16 + 32)
                        wait(pool, s.down, u + (i - 1) * s.per)
                        if s is s1 and isinstance(r, int):
                            pool.wait_ge(s0.down, s0.units)
                            pool.wait_ge(s0.split, 2 * s0.rounds)
                        wait(pool, s.split, (r + i) * 2)
                        pool.tensor_tensor(w_hi[i][:, 0:cols], raw[i][:, 0:cols],
                                           const[:, ONES:ONES + 1].broadcast_to([P, cols]), ALU.mult)\
                            .then_inc(s.split, 1)
                        pool.wait_ge(s.split, (r + i) * 2 + 1)
                        pool.tensor_tensor(w_lo[i][:, 0:cols], raw[i][:, 0:cols], w_hi[i][:, 0:cols].bitcast(F32),
                                           ALU.subtract).then_inc(s.split, 1)
                run_pairs(pool, s, body)

            def k_stack_steps():
                pool.wait_ge(k3_ready, GROUPS)
                step(pool.tensor_copy(k3_part[:, :, :, :], k3[:, :, :, :]))
                low = slice(2 * HG * D, STACK)
                step(pool.tensor_tensor(k3_part[low, :, :, :], k3[low, :, :, :], k3_part[low, :, :, :].bitcast(F32),
                                        ALU.subtract))
                for b in range(B):
                    for g in range(GROUPS):
                        step(pool.tensor_tensor(
                            k_stack[0:STACK, b, g * HG:(g + 1) * HG, :],
                            k3_part[:, g, b, :].bitcast(F32).unsqueeze(1).broadcast_to([STACK, HG, C]),
                            const[0:STACK, HMASK:HMASK + HG].unsqueeze(2).broadcast_to([STACK, HG, C]),
                            ALU.mult))
                    last = pool.tensor_copy(k_stack[STACK:P, b, :, :],
                                            const[STACK:P, HSEL:HSEL + H].unsqueeze(2).broadcast_to([P - STACK, H, C]))
                    last.then_inc(k_stack_ready, 1)
                    pool.wait_ge(k_stack_ready, b + 1)

            k_stack_steps()
            split(s0, 3 * HID0)
            split(s1, 2 * KT * P)

        def split_halves_act(act, n):
            for half in range(2):
                act.wait_ge(xT_psum, 2 * n + half + 1)
                act.activation(xT_hi[:, half * HALF:(half + 1) * HALF], bank[half][:, :], ACT.Copy)\
                    .then_inc(xT_hi_ready, 1)

        @block.scalar
        def _(act):
            act.dma_start(const[:, :], consts_in).then_inc(const_loaded, 16)
            act.dma_start(par[:, :], split_in).then_inc(par_loaded, 16)
            act.dma_start(conv_w_sb[:, :, :], conv_w.rearrange("r f o -> f r o")).then_inc(conv_loaded, 16)
            act.wait_ge(zeroed, 2)
            for b in range(B):
                act.dma_start(addend[UNITS - NCONV - P:P, b * (NT // B) + 1, :],
                              conv_b.unsqueeze(0).broadcast_to([NCONV, P])).then_inc(add_loaded, 16)
                act.dma_start(addend[T - C - 3 * P:P, b * (NT // B) + 3, :], ctx[b, :, :]).then_inc(add_loaded, 16)
            act.dma_start(rows[:, :], rows_in.broadcast_to([P, NROWS])).then_inc(rows_loaded, 16)
            act.dma_start(bqk[:, :], bqk_in).then_inc(rows_loaded, 16)

            def ln_std(n, tiles):
                act.wait_ge(var_ready, n + 1)
                act.activation(std[:, 0:tiles, :], mv[:, 0:tiles, 1:2], ACT.Sqrt, bias=eps[:, :]).then_inc(std_ready, 1)

            act.wait_ge(eps_set, 1)
            ln_std(0, NT + B)
            act.wait_ge(rows_loaded, 32)
            for g in range(GROUPS):
                act.wait_ge(k_psum, g // 2 * 2 + 2)
                act.activation(k3[:, g, :, :], bank[2 + g // 2][0:STACK, (g % 2) * B * C:(g % 2 + 1) * B * C]
                               .rearrange("p (b c) -> p b c", b=B),
                               ACT.Identity, bias=bqk[:, GROUPS + g:GROUPS + g + 1]).then_inc(k3_ready, 1)
            ln_std(1, NT)
            split_halves_act(act, 0)
            act.wait_ge(diff_ready, 1)
            act.activation(top0[:, 3, :], top0[:, 2, :], ACT.Exp).then_inc(exp_ready, 1)

            def stream(s):
                def silu(u, v):
                    wait(act, s.b_ready, u + v + 1)
                    wait(act, s.gated if s.two_gates else s.hw, u + v - 1)
                    src = bank[(2 if s.two_gates else 0) + v % 2]
                    act.activation(silu_out[:, v % 2, :], src[:, :], ACT.Silu).then_inc(s.silu, 1)

                def high(u, v):
                    wait(act, s.hw, u + v + 1)
                    wait(act, s.down, u + v + 1 - NH)
                    act.activation(h_hi[v % NH][:, :], hw[:, v % 2, :], ACT.Copy).then_inc(s.hi, 1)

                def body(u, r):
                    for v in range(2 * s.per):
                        silu(u, v)
                        if not (isinstance(u, int) and v == 0):
                            high(u, v - 1)
                run_pairs(act, s, body)
                high(s.units, -1)

            def out_halves(n):
                act.wait_ge((s0, s1)[n].down, (s0, s1)[n].units)
                act.activation(yT[:, 0:HALF], acc[0][:, :], ACT.Copy).then_inc(yT_ready, 1)

            stream(s0)
            out_halves(0)
            ln_std(2, NT)
            split_halves_act(act, 1)
            for i in range(B * GROUPS):
                g, b = i % GROUPS, i // GROUPS
                act.wait_ge(q_psum, i + 1)
                act.activation(q_stack[0:STACK, g, b * T:(b + 1) * T], bank[2 + i % 2][0:STACK, :], ACT.Identity,
                               bias=bqk[:, g:g + 1]).then_inc(q_hi_ready, 1)
            act.wait_ge(nmaxT_psum, NT // B)
            for g in range(GROUPS):
                act.activation(q_stack[STACK:P, g, 0:T], bank[0][STACK:P, :], ACT.Copy).then_inc(q_max_ready[0], 1)
            for i in range(B * H):
                act.wait_ge(scoresT_ready, i + 1)
                wait(act, pv_done, i + 1 - NE)
                act.activation(exps[:, i % NE, :], bank[i % 4][0:C, :], ACT.Exp, scale=SCALE).then_inc(exp_done, 1)
            for b in range(B):
                act.wait_ge(oT_psum, b + 1)
                act.activation(oT_hi[:, b * T:(b + 1) * T], bank[b][:, :], ACT.Copy).then_inc(oT_hi_ready, 1)
            ln_std(3, NT)
            split_halves_act(act, 2)
            act.wait_ge(lg1_ready, 1)
            act.activation(prob1[:, :, :], lg1[:, :, :], ACT.Sigmoid).then_inc(prob_ready, 1)
            for half in range(2):
                act.wait_ge(shared_gate, half + 1)
                act.activation(hw[:, half, :], bank[4 + half][:, :], ACT.Silu).then_inc(shared_silu, 1)
                act.wait_ge(shared_silu, half + 1)
                act.activation(h_hi[half][:, :], hw[:, half, :], ACT.Copy).then_inc(shared_hi, 1)
            for k in (0, 1):
                act.wait_ge(combT1_psum, k + 1)
                act.activation(combT1[:, k, :], bank[k][:, :].bitcast(BF16)[0:3 * EK, :], ACT.Copy)\
                    .then_inc(combT1_ready, 1)
            stream(s1)
            out_halves(1)

        @block.vector
        def _(dve):
            steps = [0]

            def step(ins):
                steps[0] += 1
                ins.then_inc(dve_step, 1)
                dve.wait_ge(dve_step, steps[0])

            def layer_norm(n, src, tiles):
                last = None
                for t in range(tiles):
                    last = dve.bn_stats(stats[:, t, :], src[:, t, :])
                step(last)
                for t in range(tiles):
                    last = dve.bn_aggr(mv[:, t, :], stats[:, t, :])
                last.then_inc(var_ready, 1)
                dve.wait_ge(std_ready, n + 1)
                step(dve.reciprocal(rstd[:, 0:tiles, :], std[:, 0:tiles, :]))
                order = list(range(NT, tiles)) + list(range(min(tiles, NT)))
                for t in order:
                    dve.tensor_scalar(xn[:, t, :], src[:, t, :], mv[:, t, 0:1], rstd[:, t, :], ALU.subtract, ALU.mult)\
                        .then_inc(xn_ready, 1)

            def split_halves(n):
                for half in range(2):
                    cols = slice(half * HALF, (half + 1) * HALF)
                    dve.wait_ge(xT_hi_ready, 2 * n + half + 1)
                    dve.tensor_tensor(xT_lo[:, cols], bank[half][:, :], xT_hi[:, cols].bitcast(F32), ALU.subtract)\
                        .then_inc(xT_lo_ready, 1)

            dve.wait_ge(shift_loaded, 16 * 5 * B)
            layer_norm(0, shifted, NT + B)
            dve.wait_ge(convT_psum, 1)
            dve.wait_ge(zeroed, 3)
            at = UNITS - NCONV - P
            dve.tensor_copy(conv_x[:, :, :, at:P],
                            bank[0][:, 0:B * P].rearrange("p (b m) -> p b m", b=B)[:, :, 0:CONV_ROWS]
                            .rearrange("p b (j r) -> p b r j", r=RATE)).then_inc(conv_x_ready, 1)
            dve.wait_ge(x_loaded, 16)
            dve.wait_ge(xn_ready, NT + B)
            step(dve.tensor_tensor(resid[:, :, :], resid[:, :, :], xn[:, 0:NT, :], ALU.add))
            dve.wait_ge(add_loaded, 16 * 2 * B)
            odd = resid[:, :, :].rearrange("p (n two) d -> p n two d", two=2)[:, :, 1, :]
            step(dve.tensor_tensor(odd, odd, addend[:, :, :].rearrange("p (n two) d -> p n two d", two=2)[:, :, 1, :],
                                   ALU.add))
            dve.wait_ge(conv_done, 1)
            ones4 = resid[:, :, :].rearrange("p (b n) d -> p b n d", b=B)[:, :, 1, :]
            step(dve.tensor_tensor(ones4, ones4, bank[1][:, 0:B * P].rearrange("p (b d) -> p b d", b=B), ALU.add))

            dve.wait_ge(v_psum, 1)
            dve.wait_ge(zeroed, 5)
            dve.wait_ge(rows_loaded, 32)
            for b in range(B):
                dve.tensor_tensor(v_ones[:, b, :, 0:D],
                                  bank[4][0:C, b * P:(b + 1) * P].rearrange("p (h d) -> p h d", h=H),
                                  rows[0:C, BV:BV + P].rearrange("p (h d) -> p h d", h=H), ALU.add).then_inc(v_ready, 1)

            layer_norm(1, resid, NT)
            split_halves(0)
            dve.wait_ge(logits0, 1)
            step(dve.tensor_tensor(lg0[:, :, :], bank[5][:, 0:NT * E0].rearrange("p (n e) -> p n e", n=NT),
                                   rows[:, RB0:RB0 + E0].unsqueeze(1).broadcast_to([P, NT, E0]), ALU.add))
            other = lg0[:, :, :].unsqueeze(2).broadcast_to([P, NT, E0, E0])
            own = lg0[:, :, :].unsqueeze(3).broadcast_to([P, NT, E0, E0])
            dve.tensor_tensor(pair_gt[:, :, :, :], other, own, ALU.is_gt)
            step(dve.tensor_tensor(pair_eq[:, :, :, :], other, own, ALU.is_equal))
            flat = "p n a b -> p n (a b)"
            dve.wait_ge(const_loaded, 16)
            step(dve.tensor_tensor(pair_eq[:, :, :, :].rearrange(flat), pair_eq[:, :, :, :].rearrange(flat),
                                   const[:, TRI:TRI + E0 * E0].unsqueeze(1).broadcast_to([P, NT, E0 * E0]), ALU.mult))
            step(dve.tensor_tensor(pair_gt[:, :, :, :], pair_gt[:, :, :, :], pair_eq[:, :, :, :], ALU.add))
            step(dve.tensor_reduce(rank0[:, :, :], pair_gt[:, :, :, :], AX.X, ALU.add))
            step(dve.tensor_scalar(chosen0[:, :, :], rank0[:, :, :], 2.0, None, ALU.is_lt))
            dve.tensor_scalar(second0[:, :, :], rank0[:, :, :], 1.0, None, ALU.is_equal).then_inc(chosen_ready, 1)
            dve.tensor_scalar(first0[:, :, :], rank0[:, :, :], 0.0, None, ALU.is_equal)
            step(dve.tensor_reduce(top0[:, 0, :], lg0[:, :, :], AX.X, ALU.max))
            step(dve.tensor_tensor(tmp0[:, :, :], lg0[:, :, :], second0[:, :, :], ALU.mult))
            step(dve.tensor_reduce(top0[:, 1, :], tmp0[:, :, :], AX.X, ALU.add))
            dve.tensor_tensor(top0[:, 2, :], top0[:, 1, :], top0[:, 0, :], ALU.subtract).then_inc(diff_ready, 1)
            dve.wait_ge(exp_ready, 1)
            step(dve.tensor_scalar(top0[:, 4, :], top0[:, 3, :], 1.0, None, ALU.add))
            step(dve.reciprocal(top0[:, 4, :], top0[:, 4, :]))
            step(dve.tensor_tensor(top0[:, 5, :], top0[:, 3, :], top0[:, 4, :], ALU.mult))
            step(dve.tensor_tensor(first0[:, :, :], first0[:, :, :],
                                   top0[:, 4, :].unsqueeze(2).broadcast_to([P, NT, E0]), ALU.mult))
            step(dve.tensor_tensor(second0[:, :, :], second0[:, :, :],
                                   top0[:, 5, :].unsqueeze(2).broadcast_to([P, NT, E0]), ALU.mult))
            step(dve.tensor_tensor(comb0[:, :, :], first0[:, :, :], second0[:, :, :], ALU.add))
            dve.wait_ge(place_ready, 1)
            step(dve.scalar_tensor_tensor(comb0[:, :, :], bank[4][:, 256:256 + NT * E0].rearrange("p (n e) -> p n e", n=NT),
                                          float(CAPACITY), comb0[:, :, :], ALU.is_lt, ALU.mult))

            def three_parts(src, dst, rest):
                step(dve.tensor_copy(dst(0), src))
                step(dve.tensor_tensor(rest, src, dst(0), ALU.subtract))
                step(dve.tensor_copy(dst(1), rest))
                return dve.tensor_tensor(dst(2), rest, dst(1), ALU.subtract)

            three_parts(comb0[:, :, :], lambda j: parts0[:, :, j, :], tmp0[:, :, :]).then_inc(parts0_ready, 1)
            dve.wait_ge(combT0_psum, 1)
            dve.tensor_copy(combT0[:, :], bank[0][:, :].bitcast(BF16)[0:3 * E0, :]).then_inc(combT0_ready, 1)

            def stream(s):
                def multiply(u, v):
                    i = v % 2
                    c = bank[(4 if s.two_gates else 2) + i]
                    wait(dve, s.silu, u + v + 1)
                    src = silu_out[:, i, :]
                    if s.two_gates:
                        wait(dve, s.a_ready, u + v + 1)
                        dve.tensor_tensor(gated[:, i, :], src, bank[i][:, :], ALU.mult).then_inc(s.gated, 1)
                        wait(dve, s.gated, u + v + 1)
                        src = gated[:, i, :]
                    wait(dve, s.c_ready, u + v + 1)
                    wait(dve, s.hi, u + v - 1)
                    wait(dve, s.lo, u + v - 1)
                    dve.tensor_tensor(hw[:, i, :], src, c[:, :], ALU.mult).then_inc(s.hw, 1)

                def low(u, v):
                    wait(dve, s.hi, u + v + 1)
                    dve.tensor_tensor(h_lo[v % NH][:, :], hw[:, v % 2, :], h_hi[v % NH][:, :].bitcast(F32),
                                      ALU.subtract).then_inc(s.lo, 1)

                def body(u, r):
                    for v in range(2 * s.per):
                        multiply(u, v)
                        if not (isinstance(u, int) and v == 0):
                            low(u, v - 1)
                run_pairs(dve, s, body)
                low(s.units, -1)

            def add_back(n, ready):
                dve.wait_ge((s0, s1)[n].down, (s0, s1)[n].units)
                dve.tensor_copy(yT[:, HALF:2 * HALF], acc[1][:, :]).then_inc(yT_ready, 1)
                for half in range(2):
                    part = resid[:, half * NT // 2:(half + 1) * NT // 2, :]
                    dve.wait_ge(y_psum, 2 * n + half + 1)
                    ready(dve.tensor_tensor(part, part, bank[half][:, :].rearrange("p (n d) -> p n d", d=P), ALU.add))

            stream(s0)
            add_back(0, step)

            layer_norm(2, resid, NT)
            split_halves(1)
            step(dve.tensor_tensor(resid[:, :, :], resid[:, :, :],
                                   rows[:, BO:BO + P].unsqueeze(1).broadcast_to([P, NT, P]), ALU.add))
            mid = slice(HG * D, 2 * HG * D)
            for i in range(B * GROUPS):
                g, b = i % GROUPS, i // GROUPS
                dve.wait_ge(q_hi_ready, i + 1)
                dst = q_stack[mid, g, b * T:(b + 1) * T]
                dve.scalar_tensor_tensor(dst, bank[2 + i % 2][mid, :], bqk[mid, g:g + 1], dst.bitcast(F32),
                                         ALU.add, ALU.subtract).then_inc(q_lo_ready, 1)
            for t in range(NT):
                for pair in range(2):
                    n = 2 * t + pair
                    dve.wait_ge(scores_ready, n + 1)
                    last = None
                    for k in range(2):
                        last = dve.tensor_reduce(
                            nmax[:, t % 2, (2 * pair + k) * HG:(2 * pair + k + 1) * HG],
                            bank[4 + 2 * pair + k][:, 0:HG * C].rearrange("p (h c) -> p h c", h=HG),
                            AX.X, ALU.max, negate=True)
                    step(last)
                wait(dve, nmaxT_psum, t - 1)
                dst = nmax_pad[:, t % 2, STACK:STACK + H]
                step(dve.tensor_copy(dst.bitcast(F32R), nmax[:, t % 2, :]))
                dve.tensor_tensor(nmax_pad[:, t % 2, STACK + H:P].bitcast(F32R), nmax[:, t % 2, :], dst, ALU.subtract)\
                    .then_inc(nmax_ready, 1)
            dve.wait_ge(nmaxT_psum, NT)
            for g in range(GROUPS):
                dve.tensor_copy(q_stack[STACK:P, g, T:2 * T], bank[1][STACK:P, :]).then_inc(q_max_ready[1], 1)
            for b in range(B):
                dve.wait_ge(pv_done, (b + 1) * H)
                for k in range(2):
                    t0 = b * (NT // B) + 2 * k
                    pv = bank[4 + 2 * b + k][:, 0:2 * H * (D + 1)].rearrange("p (t h d) -> p t h d", t=2, h=H)
                    step(dve.reciprocal(inv[:, t0:t0 + 2, :], pv[:, :, :, D]))
                    for t in range(2):
                        dve.tensor_tensor(onat[:, t0 + t, :].rearrange("p (h d) -> p h d", h=H), pv[:, t, :, 0:D],
                                          inv[:, t0 + t, :].unsqueeze(2).broadcast_to([P, H, D]), ALU.mult)\
                            .then_inc(onat_ready, 1)
            for b in range(B):
                cols = slice(b * T, (b + 1) * T)
                dve.wait_ge(oT_hi_ready, b + 1)
                dve.tensor_tensor(oT_lo[:, cols], bank[b][:, :], oT_hi[:, cols].bitcast(F32), ALU.subtract)\
                    .then_inc(oT_lo_ready, 1)
            for b in range(B):
                part = resid[:, b * NT // B:(b + 1) * NT // B, :]
                dve.wait_ge(proj_done, b + 1)
                step(dve.tensor_tensor(part, part, bank[2 + b][:, :].rearrange("p (n d) -> p n d", d=P), ALU.add))

            layer_norm(3, resid, NT)
            split_halves(2)
            for k, (t0, t1) in enumerate(((0, 3), (3, 6), (6, 8))):
                dve.wait_ge(logits1, k + 1)
                last = dve.tensor_tensor(lg1[:, t0:t1, :],
                                         bank[2 + k if k < 2 else 6][:, 0:(t1 - t0) * E1].rearrange("p (n e) -> p n e", e=E1),
                                         rows[:, EB:EB + E1].unsqueeze(1).broadcast_to([P, t1 - t0, E1]), ALU.add)
            last.then_inc(lg1_ready, 1)
            dve.wait_ge(lg1_ready, 1)
            step(dve.tensor_scalar(key1[:, :, :], lg1[:, :, :], SIG_LOW, SIG_HIGH, ALU.max, ALU.min))
            for half in range(2):
                dve.wait_ge(shared_hi, half + 1)
                dve.tensor_tensor(h_lo[half][:, :], hw[:, half, :], h_hi[half][:, :].bitcast(F32), ALU.subtract)\
                    .then_inc(shared_lo, 1)
            last = None
            for t in range(NT):
                last = dve.max(best1[:, t, :], key1[:, t, :])
            step(last)
            for t in range(NT):
                last = dve.match_replace(key1[:, t, :], best1[:, t, :], key1[:, t, :], -3e38)
            step(last)
            dve.wait_ge(prob_ready, 1)
            for t in range(NT):
                last = dve.scalar_tensor_tensor(comb1[:, t, :], key1[:, t, :], -1e38, prob1[:, t, :],
                                                ALU.is_lt, ALU.mult, accum_out=sum1[:, t:t + 1])
            step(last)
            step(dve.tensor_scalar(sum1[:, :], sum1[:, :], 1e-9, None, ALU.add))
            step(dve.reciprocal(sum1[:, :], sum1[:, :]))
            for t in range(NT):
                last = dve.tensor_scalar(comb1[:, t, :], comb1[:, t, :], sum1[:, t:t + 1], ROUTED_SCALE,
                                         ALU.mult, ALU.mult)
            step(last)
            by_k = "p n (k e) -> p n k e"
            three_parts(comb1[:, :, :].rearrange(by_k, k=KT), lambda j: parts1[:, :, :, j, :],
                        lg1[:, :, :].rearrange(by_k, k=KT)).then_inc(parts1_ready, 1)
            for k in (2, 3):
                dve.wait_ge(combT1_psum, k + 1)
                dve.tensor_copy(combT1[:, k, :], bank[k][:, :].bitcast(BF16)[0:3 * EK, :]).then_inc(combT1_ready, 1)
            stream(s1)
            add_back(1, lambda ins: ins.then_inc(out_ready, 1))

        @block.tensor
        def _(pe):
            mm = nc.tensor.matmul

            def three(dst, w, rhs, start, stop):
                (wh, wl), (rh, rl) = w, rhs
                mm(dst, wh, rh, start=start, stop=False)
                mm(dst, wh, rl, start=False, stop=False)
                return mm(dst, wl, rh, start=False, stop=stop)

            def cols(half):
                c = slice(half * HALF, (half + 1) * HALF)
                return xT_hi[:, c], xT_lo[:, c]

            def tile_of(t):
                c = slice(t * P, (t + 1) * P)
                return xT_hi[:, c], xT_lo[:, c]

            def transpose_rows(n, before):
                for t in range(NT):
                    pe.wait_ge(xn_ready, before + t + 1)
                    last = nc.tensor.transpose(bank[t // 4][:, (t % 4) * P:(t % 4 + 1) * P], xn[:, t, :], ident)
                    if t % 4 == 3:
                        last.then_inc(xT_psum, 1)

            pe.wait_ge(const_loaded, 16)
            for b in range(B):
                pe.wait_ge(xn_ready, b + 1)
                last = nc.tensor.transpose(bank[0][:, b * P:(b + 1) * P], xn[:, NT + b, :], ident)
            last.then_inc(convT_psum, 1)
            pe.wait_ge(conv_x_ready, 1)
            pe.wait_ge(conv_loaded, 16)
            for b in range(B):
                for r in range(RATE):
                    last = mm(bank[1][:, b * P:(b + 1) * P], conv_x[:, b, r, :], conv_w_sb[:, r, :],
                              start=r == 0, stop=r == RATE - 1)
            last.then_inc(conv_done, 1)
            pe.wait_ge(par_split, 2)
            for g in range(GROUPS):
                c = (g * STACK, (g + 1) * STACK)
                three(bank[2 + g // 2][0:STACK, (g % 2) * B * C:(g % 2 + 1) * B * C],
                      (hi("wk", *c), lo("wk", *c)), (hi("ctxT"), lo("ctxT")), True, True).then_inc(k_psum, 1)
            for b in range(B):
                c = (b * C, (b + 1) * C)
                last = three(bank[4][0:C, b * P:(b + 1) * P], (hi("ctxT", *c), lo("ctxT", *c)), (hi("wv"), lo("wv")),
                             True, True)
            last.then_inc(v_psum, 1)

            pe.wait_ge(x_loaded, 16)
            pe.wait_ge(conv_x_ready, 1)
            transpose_rows(0, NT + B)
            for t in range(NT):
                pe.wait_ge(xT_lo_ready, t // 4 + 1)
                last = three(bank[5][:, t * E0:(t + 1) * E0], tile_of(t), (hi("rw0"), lo("rw0")), True, True)
            last.then_inc(logits0, 1)
            pe.wait_ge(chosen_ready, 1)
            pe.wait_ge(v_ready, B)
            place = bank[4][:, 256:256 + NT * E0]
            picks = chosen0[:, :, :].rearrange("p n e -> p (n e)")
            mm(place, const[:, ULT:ULT + P], picks, start=True, stop=False)
            for d in range(1, NT):
                last = mm(place[:, d * E0:], const[:, ONES:ONES + P], picks[:, 0:(NT - d) * E0], start=False,
                          stop=d == NT - 1)
            last.then_inc(place_ready, 1)
            pe.wait_ge(parts0_ready, 1)
            pe.wait_ge(ident_cast, 1)
            for t in range(NT):
                last = nc.tensor.transpose(bank[0][:, :].bitcast(BF16)[0:3 * E0, t * P:(t + 1) * P],
                                           parts0[:, t, :, :].rearrange("p j e -> p (j e)"), ident_bf[:, :])
            last.then_inc(combT0_psum, 1)

            def stream(s, opened):
                def up(u, r, v):
                    slot, i = v // s.per, v % 2
                    gate, lin, _, pick, comb, half = operands(s, v % s.per, slot)
                    if v % s.per == 0:
                        pe.wait_ge(s.split, (r + slot) * 2 + 2)
                    wait(pe, s.silu, u + v - 1)
                    three(bank[(2 if s.two_gates else 0) + i][:, :], (w_hi[slot][:, gate], w_lo[slot][:, gate]), cols(half),
                          True, True).then_inc(s.b_ready, 1)
                    if s.two_gates:
                        wait(pe, s.gated, u + v - 1)
                        three(bank[i][:, :], (w_hi[slot][:, lin], w_lo[slot][:, lin]), cols(half), True, True)\
                            .then_inc(s.a_ready, 1)
                    if v % s.per == 0:
                        pe.wait_ge(s.loaded[slot], r * 16 + 32)
                    wait(pe, s.hw, u + v - 1)
                    mm(bank[(4 if s.two_gates else 2) + i][:, :], pick, comb, start=True, stop=True).then_inc(s.c_ready, 1)

                def down(u, v, first=False, last=False):
                    slot = (v // s.per) % 2
                    _, _, cols_down, _, _, half = operands(s, v % s.per, slot)
                    wait(pe, s.lo, u + v + 1)
                    three(acc[half][:, :], (w_hi[slot][:, cols_down], w_lo[slot][:, cols_down]),
                          (h_hi[v % NH][:, :], h_lo[v % NH][:, :]), first, last).then_inc(s.down, 1)

                def body(u, r):
                    for v in range(2 * s.per):
                        up(u, r, v)
                        if not isinstance(u, int) or v >= s.lag:
                            down(u, v - s.lag, first=isinstance(u, int) and v - s.lag < 2 and not opened)
                run_pairs(pe, s, body)
                for v in range(-s.lag, 0):
                    down(s.units, v, last=v >= -2)

            def transpose_back(n):
                pe.wait_ge(yT_ready, 2 * n + 2)
                for t in range(NT):
                    last = nc.tensor.transpose(bank[t // 4][:, (t % 4) * P:(t % 4 + 1) * P], yT[:, t * P:(t + 1) * P],
                                               ident)
                    if t % 4 == 3:
                        last.then_inc(y_psum, 1)

            pe.wait_ge(combT0_ready, 1)
            stream(s0, False)
            transpose_back(0)

            transpose_rows(1, 2 * NT + B)
            for i in range(B * GROUPS):
                g, b = i % GROUPS, i // GROUPS
                c = (g * STACK, (g + 1) * STACK)
                pe.wait_ge(xT_lo_ready, 2 + b + 1)
                wait(pe, q_lo_ready, i - 1)
                three(bank[2 + i % 2][0:STACK, :], (hi("wq", *c), lo("wq", *c)), cols(b), True, True).then_inc(q_psum, 1)
            pe.wait_ge(k_stack_ready, B)

            def turn_max(t):
                pe.wait_ge(nmax_ready, t + 1)
                nc.tensor.transpose(bank[t // 4][:, (t % 4) * P:(t % 4 + 1) * P], nmax_pad[:, t % 2, :], ident)\
                    .then_inc(nmaxT_psum, 1)

            for t in range(NT):
                b = t // (NT // B)
                pe.wait_ge(q_lo_ready, (b + 1) * GROUPS)
                for pair in range(2):
                    wait(pe, nmax_ready, t)
                    for k in range(2):
                        g = 2 * pair + k
                        last = mm(bank[4 + g][:, 0:HG * C], q_stack[0:STACK, g, t * P:(t + 1) * P],
                                  k_stack[0:STACK, b, g * HG:(g + 1) * HG, :].rearrange("p h c -> p (h c)"),
                                  start=True, stop=True)
                    last.then_inc(scores_ready, 1)
                if t >= 1:
                    turn_max(t - 1)
            turn_max(NT - 1)

            def values(i):
                b, h = divmod(i, H)
                pe.wait_ge(exp_done, i + 1)
                for t in range(NT // B):
                    at = ((t % 2) * H + h) * (D + 1)
                    last = mm(bank[4 + 2 * b + t // 2][:, at:at + D + 1], exps[:, i % NE, t * P:(t + 1) * P],
                              v_ones[:, b, h, :], start=True, stop=True)
                last.then_inc(pv_done, 1)

            for b in range(B):
                pe.wait_ge(q_max_ready[b], GROUPS)
            for i in range(B * H):
                b, h = divmod(i, H)
                wait(pe, exp_done, i - 3)
                mm(bank[i % 4][0:C, :], k_stack[:, b, h, :], q_stack[:, h // HG, b * T:(b + 1) * T],
                   start=True, stop=True).then_inc(scoresT_ready, 1)
                if i >= 2:
                    values(i - 2)
            values(B * H - 2)
            values(B * H - 1)
            for b in range(B):
                for t in range(NT // B):
                    n = b * (NT // B) + t
                    pe.wait_ge(onat_ready, n + 1)
                    last = nc.tensor.transpose(bank[b][:, t * P:(t + 1) * P], onat[:, n, :], ident)
                last.then_inc(oT_psum, 1)
            for b in range(B):
                pe.wait_ge(oT_lo_ready, b + 1)
                for t in range(NT // B):
                    c = slice((b * (NT // B) + t) * P, (b * (NT // B) + t + 1) * P)
                    last = three(bank[2 + b][:, t * P:(t + 1) * P], (oT_hi[:, c], oT_lo[:, c]), (hi("wo"), lo("wo")),
                                 True, True)
                last.then_inc(proj_done, 1)

            transpose_rows(2, 3 * NT + B)
            for k, (t0, t1) in enumerate(((0, 3), (3, 6), (6, 8))):
                for t in range(t0, t1):
                    pe.wait_ge(xT_lo_ready, 4 + t // 4 + 1)
                    last = three(bank[2 + k if k < 2 else 6][:, (t - t0) * E1:(t - t0 + 1) * E1], tile_of(t),
                                 (hi("rw1"), lo("rw1")), True, True)
                last.then_inc(logits1, 1)
            for half in range(2):
                three(bank[4 + half][:, :], (hi("wgs"), lo("wgs")), cols(half), True, True).then_inc(shared_gate, 1)
            pe.wait_ge(lg1_ready, 1)
            for half in range(2):
                pe.wait_ge(shared_lo, half + 1)
                three(acc[half][:, :], (hi("wds"), lo("wds")), (h_hi[half][:, :], h_lo[half][:, :]), True, False)\
                    .then_inc(shared_down, 1)
            pe.wait_ge(parts1_ready, 1)
            for k in range(KT):
                for t in range(NT):
                    last = nc.tensor.transpose(bank[k][:, :].bitcast(BF16)[0:3 * EK, t * P:(t + 1) * P],
                                               parts1[:, t, k, :, :].rearrange("p j e -> p (j e)"), ident_bf[:, :])
                last.then_inc(combT1_psum, 1)
            pe.wait_ge(combT1_ready, KT)
            stream(s1, True)
            transpose_back(1)


def kernel(x, ctx_1024, L0_xattn_conv_w, L0_xattn_conv_b, L0_ffn_router_w, L0_ffn_router_b, L0_ffn_W, L0_ffn_V,
           L0_ffn_W_out, L1_xattn_Wq, L1_xattn_bq, L1_xattn_Wk, L1_xattn_bk, L1_xattn_Wv, L1_xattn_bv, L1_xattn_Wo,
           L1_xattn_bo, L1_ffn_router_w, L1_ffn_expert_bias, L1_ffn_w_gate, L1_ffn_w_down, L1_ffn_w_gate_shared,
           L1_ffn_w_down_shared):
    import numpy as np
    import concourse.bacc as bacc
    from concourse.bass_utils import run_bass_kernel_spmd

    def arr(a):
        return np.asarray(a)

    def stacked(w):
        g = arr(w).T.reshape(P, GROUPS, HG * D)
        return np.concatenate([g, g, g], axis=2).reshape(P, GROUPS * STACK)

    def stacked_bias(v):
        g = arr(v).reshape(GROUPS, HG * D).T
        return np.concatenate([g, g, g], axis=0)

    f32 = np.float32
    ctx = arr(ctx_1024)
    shared_gate = np.concatenate([arr(L1_ffn_w_gate_shared).T, np.zeros((P, P - INTER), f32)], axis=1)
    shared_down = np.concatenate([arr(L1_ffn_w_down_shared).T, np.zeros((P - INTER, P), f32)], axis=0)
    columns = {"rw0": arr(L0_ffn_router_w).T, "ctxT": ctx.reshape(B * C, P).T, "wk": stacked(L1_xattn_Wk),
               "wv": arr(L1_xattn_Wv).T, "wq": stacked(L1_xattn_Wq), "wo": arr(L1_xattn_Wo).T,
               "rw1": arr(L1_ffn_router_w).T, "wgs": shared_gate, "wds": shared_down}
    split_in = np.concatenate([columns[n] for n in SPLIT], axis=1)
    rows_in = np.concatenate([arr(L0_ffn_router_b), arr(L1_xattn_bv), arr(L1_xattn_bo), arr(L1_ffn_expert_bias)])[None, :]
    bqk_in = np.concatenate([stacked_bias(L1_xattn_bq), stacked_bias(L1_xattn_bk)], axis=1)
    w0_in = np.concatenate([arr(L0_ffn_W), arr(L0_ffn_V),
                            arr(L0_ffn_W_out).reshape(E0, HID0 // P, P, P).transpose(0, 2, 1, 3).reshape(E0, P, HID0)],
                           axis=2)
    gate = arr(L1_ffn_w_gate).reshape(KT, ROUNDS1, 2, INTER, P).transpose(1, 4, 0, 2, 3).reshape(ROUNDS1, P, KT * P)
    down = arr(L1_ffn_w_down).reshape(KT, ROUNDS1, 2, P, INTER).transpose(1, 2, 4, 0, 3).reshape(ROUNDS1, P, KT * P)
    w1_in = np.concatenate([gate, down], axis=2)

    consts_in = np.zeros((P, NCONST), f32)
    i = np.arange(P)
    consts_in[:, IDENT:IDENT + P] = np.eye(P, dtype=f32)
    consts_in[:, ULT:ULT + P] = i[:, None] < i[None, :]
    consts_in[:, ONES:ONES + P] = 1
    e = np.arange(E0)
    consts_in[:, TRI:TRI + E0 * E0] = (e[None, :] < e[:, None]).reshape(1, E0 * E0)
    for j in range(HG):
        consts_in[:, HMASK + j] = (i % (HG * D)) // D == j
    for h in range(H):
        consts_in[STACK + h, HSEL + h] = 1
        consts_in[STACK + H + h, HSEL + h] = 1
    one = 0x3F80
    sel0_in = np.zeros((E0, 3 * E0, P), np.uint16)
    for n in range(E0):
        sel0_in[n, n::E0, :] = one
    sel1_in = np.zeros((ROUNDS1, 3 * EK, P), np.uint16)
    for r in range(ROUNDS1):
        sel1_in[r, 2 * r::EK, 0:INTER] = one
        sel1_in[r, 2 * r + 1::EK, INTER:P] = one

    arrays = {"x": arr(x), "ctx": ctx, "conv_w": arr(L0_xattn_conv_w), "conv_b": arr(L0_xattn_conv_b),
              "split_in": split_in, "consts_in": consts_in, "rows_in": rows_in, "bqk_in": bqk_in, "w0_in": w0_in,
              "sel0_in": sel0_in, "w1_in": w1_in, "sel1_in": sel1_in}
    arrays = {n: np.ascontiguousarray(a) for n, a in arrays.items()}
    nc = bacc.Bacc("TRN2", target_bir_lowering=False, num_devices=1)
    args = [nc.dram_tensor(n, a.shape, mybir.dt.from_np(a.dtype), kind="ExternalInput").ap() for n, a in arrays.items()]
    out = nc.dram_tensor("out", (B, T, P), F32, kind="ExternalOutput").ap()
    build_program(nc, *args, out)
    result = run_bass_kernel_spmd(nc, [arrays], core_ids=[0])
    return result.results[0]["out"]
```

```python
import concourse.bass as bass
from concourse import mybir
from contextlib import ExitStack

F32 = mybir.dt.float32
F32R = mybir.dt.float32r
BF16 = mybir.dt.bfloat16
ALU = mybir.AluOpType
ACT = mybir.ActivationFunctionType
AX = mybir.AxisListType

P = 128
B, T, C = 2, 512, 77
NT = B * T // P
HALF = 512
EPS = 1e-5
UNITS, RATE = 256, 4
NCONV = (C - RATE) // RATE + 1
CONV_ROWS = NCONV * RATE
E0, HID0, CAPACITY = 8, 256, 256
H, D = 16, 8
GROUPS, HG = 4, 4
STACK = 3 * HG * D
SCALE = D ** -0.5
E1, INTER, TOP, ROUTED_SCALE = 160, 64, 8, 2.5
ROW_GROUPS, KT = 4, 4
EC = E1 // (ROW_GROUPS * KT)
CELL = 32
ROUNDS1 = E1 // (2 * ROW_GROUPS)
SIG_LOW, SIG_HIGH = -88.72, 17.33

SPLIT = {}
_at = 0
for _name, _n in (("rw0", E0), ("ctxT", B * C), ("wk", GROUPS * STACK), ("wv", P), ("wq", GROUPS * STACK),
                  ("wo", P), ("rw1", E1), ("wgs", P), ("wds", P)):
    SPLIT[_name] = (_at, _at + _n)
    _at += _n
NSPLIT = _at
IDENT, ULT, ONES, TRI, HMASK, HSEL = 0, P, 2 * P, 3 * P, 3 * P + 64, 3 * P + 68
NCONST = 3 * P + 84
RB0, BV, BO, EB = 0, E0, E0 + P, E0 + 2 * P
NROWS = E0 + 2 * P + E1


def build_program(nc, x, ctx, conv_w, conv_b, split_in, consts_in, rows_in, bqk_in, w0_in, sel0_in, w1_in, sel1_in, out):
    stack = ExitStack()
    with stack:
        def sb(name, shape, dt=F32):
            return stack.enter_context(nc.sbuf_tensor(name, shape, dt))

        def sem(name):
            return stack.enter_context(nc.semaphore(name))

        resid = sb("resid", [P, NT, P])
        shifted = sb("shifted", [P, NT + B, P])
        addend = sb("addend", [P, NT, P])
        xn = sb("xn", [P, NT + B, P])
        stats = sb("stats", [P, NT + B, 6])
        mv = sb("mv", [P, NT + B, 2])
        std = sb("std", [P, NT + B, 1])
        rstd = sb("rstd", [P, NT + B, 1])
        xT_hi = sb("xT_hi", [P, NT * P], F32R)
        xT_lo = sb("xT_lo", [P, NT * P], F32R)
        conv_w_sb = sb("conv_w_sb", [P, RATE, P])
        conv_x = sb("conv_x", [P, B, RATE, P])
        par = sb("par", [P, NSPLIT])
        par_hi = sb("par_hi", [P, NSPLIT], F32R)
        par_lo = sb("par_lo", [P, NSPLIT], F32R)
        const = sb("const", [P, NCONST])
        ident_bf = sb("ident_bf", [P, P], BF16)
        rows = sb("rows", [P, NROWS])
        bqk = sb("bqk", [STACK, 2 * GROUPS])
        eps = sb("eps", [P, 1])
        lg0 = sb("lg0", [P, NT, E0])
        pair_gt = sb("pair_gt", [P, NT, E0, E0])
        pair_eq = sb("pair_eq", [P, NT, E0, E0])
        rank0 = sb("rank0", [P, NT, E0])
        first0 = sb("first0", [P, NT, E0])
        second0 = sb("second0", [P, NT, E0])
        chosen0 = sb("chosen0", [P, NT, E0])
        comb0 = sb("comb0", [P, NT, E0])
        tmp0 = sb("tmp0", [P, NT, E0])
        top0 = sb("top0", [P, 6, NT])
        parts0 = sb("parts0", [P, NT, 3, E0], BF16)
        combT0 = sb("combT0", [3 * E0, NT * P], BF16)
        gate1 = sb("gate1", [P, 4, NT, E1])
        lg1, key1, prob1, comb1 = (gate1[:, i, :, :] for i in range(4))
        best1 = sb("best1", [P, NT, TOP])
        sum1 = sb("sum1", [P, NT])
        parts1 = sb("parts1", [P, NT, KT * ROW_GROUPS, CELL], BF16)
        combT1 = sb("combT1", [P, KT, NT * P], BF16)
        k3 = sb("k3", [STACK, GROUPS, B, C])
        k3_part = sb("k3_part", [STACK, GROUPS, B, C], F32R)
        k_stack = sb("k_stack", [P, B, H, C], F32R)
        v_ones = sb("v_ones", [C, B, H, CELL])
        q_stack = sb("q_stack", [P, GROUPS, NT * P], F32R)
        nmax = sb("nmax", [P, NT, H])
        nmax_pad = sb("nmax_pad", [P, 2, P])
        NE = 8
        exps = gate1[0:C, :, :, :].rearrange("p a n e -> p (a n e)")[:, 0:NE * HALF]\
            .rearrange("p (i q) -> p i q", i=NE)
        pv_sb = sb("pv_sb", [P, 2, HALF])
        inv = sb("inv", [P, 2, NT // B, HG])
        onat = sb("onat", [P, NT, P])
        oT_hi = sb("oT_hi", [P, NT * P], F32R)
        oT_lo = sb("oT_lo", [P, NT * P], F32R)
        raw = [sb(f"raw{s}", [P, 1024]) for s in range(2)]
        w_hi = [sb(f"w_hi{s}", [P, 1024], F32R) for s in range(2)]
        w_lo = [sb(f"w_lo{s}", [P, 1024], F32R) for s in range(2)]
        sel = [sb(f"sel{s}", [P, P], BF16) for s in range(2)]
        silu_out = sb("silu_out", [P, 2, HALF])
        gated = sb("gated", [P, 2, HALF])
        hw = sb("hw", [P, 2, HALF])
        NH = 4
        h_hi = [sb(f"h_hi{i}", [P, HALF], F32R) for i in range(NH)]
        h_lo = [sb(f"h_lo{i}", [P, HALF], F32R) for i in range(NH)]
        yT = shifted[:, 0:NT, :].rearrange("p n d -> p (n d)")

        psum = stack.enter_context(nc.psum_tensor("psum", [P, 8, HALF], F32))
        bank = [psum[:, i, :] for i in range(8)]
        acc = bank[6:8]

        def hi(name, a=0, b=None):
            s, e = SPLIT[name]
            return par_hi[:, s + a:(e if b is None else s + b)]

        def lo(name, a=0, b=None):
            s, e = SPLIT[name]
            return par_lo[:, s + a:(e if b is None else s + b)]

        ident = const[:, IDENT:IDENT + P]

        zeroed = sem("zeroed")
        x_loaded = sem("x_loaded")
        shift_loaded = sem("shift_loaded")
        add_loaded = sem("add_loaded")
        conv_loaded = sem("conv_loaded")
        par_loaded = sem("par_loaded")
        const_loaded = sem("const_loaded")
        rows_loaded = sem("rows_loaded")
        eps_set = sem("eps_set")
        par_hi_ready = sem("par_hi_ready")
        par_lo_ready = sem("par_lo_ready")
        ident_cast = sem("ident_cast")
        dve_step = sem("dve_step")
        pool_step = sem("pool_step")
        var_ready = sem("var_ready")
        std_ready = sem("std_ready")
        xn_ready = sem("xn_ready")
        xT_psum = sem("xT_psum")
        xT_hi_ready = sem("xT_hi_ready")
        xT_lo_ready = sem("xT_lo_ready")
        convT_psum = sem("convT_psum")
        conv_x_ready = sem("conv_x_ready")
        conv_done = sem("conv_done")
        logits0 = sem("logits0")
        diff_ready = sem("diff_ready")
        exp_ready = sem("exp_ready")
        chosen_ready = sem("chosen_ready")
        place_ready = sem("place_ready")
        parts0_ready = sem("parts0_ready")
        combT0_psum = sem("combT0_psum")
        combT0_ready = sem("combT0_ready")
        k_psum = sem("k_psum")
        v_psum = sem("v_psum")
        k3_ready = sem("k3_ready")
        k_stack_ready = sem("k_stack_ready")
        v_ready = sem("v_ready")
        q_psum = sem("q_psum")
        q_hi_ready = sem("q_hi_ready")
        q_lo_ready = sem("q_lo_ready")
        scores_ready = sem("scores_ready")
        max_taken = sem("max_taken")
        nmax_ready = sem("nmax_ready")
        nmaxT_psum = sem("nmaxT_psum")
        q_max_ready = [sem(f"q_max_ready{b}") for b in range(B)]
        scoresT_ready = sem("scoresT_ready")
        exp_done = sem("exp_done")
        pv_done = sem("pv_done")
        pv_copied = sem("pv_copied")
        pv_turned = sem("pv_turned")
        onat_ready = sem("onat_ready")
        oT_psum = sem("oT_psum")
        oT_hi_ready = sem("oT_hi_ready")
        oT_lo_ready = sem("oT_lo_ready")
        proj_done = sem("proj_done")
        logits1 = sem("logits1")
        lg1_ready = sem("lg1_ready")
        prob_ready = sem("prob_ready")
        parts1_ready = sem("parts1_ready")
        combT1_psum = sem("combT1_psum")
        combT1_ready = sem("combT1_ready")
        shared_gate = sem("shared_gate")
        shared_silu = sem("shared_silu")
        shared_hi = sem("shared_hi")
        shared_lo = sem("shared_lo")
        sum_done = sem("sum_done")
        yT_ready = [sem(f"yT_ready{i}") for i in range(2)]
        y_psum = sem("y_psum")
        out_ready = sem("out_ready")
        stored = sem("stored")

        class Stream:

            def __init__(self, tag, rounds, per, body, batch, two_gates, lag):
                self.tag, self.rounds, self.per, self.body, self.batch = tag, rounds, per, body, batch
                self.two_gates, self.lag = two_gates, lag
                self.units = rounds * per
                self.loaded = [sem(f"l{tag}_loaded{s}") for s in range(2)]
                self.up_split = sem(f"l{tag}_up_split")
                self.down_split = sem(f"l{tag}_down_split")
                self.b_ready = sem(f"l{tag}_b_ready")
                self.a_ready = sem(f"l{tag}_a_ready")
                self.c_ready = sem(f"l{tag}_c_ready")
                self.silu = sem(f"l{tag}_silu")
                self.gated = sem(f"l{tag}_gated")
                self.hw = sem(f"l{tag}_hw")
                self.hi = sem(f"l{tag}_hi")
                self.lo = sem(f"l{tag}_lo")
                self.down = sem(f"l{tag}_down")

            def run(self, eng, body, rounds_per_body=None):
                body(0)
                with eng.Fori(1, self.rounds // (rounds_per_body or self.body)) as j:
                    body(j)

        s0 = Stream(0, E0, 2 * (HID0 // P), 2, HID0 // P, True, 3)
        s1 = Stream(1, ROUNDS1, 2 * ROW_GROUPS, KT, 2, False, 3)

        s0.up_read, s1.up_read = s0.a_ready, s1.b_ready
        s0.complete = (s0.down, s0.units)
        s1.complete = (sum_done, 1)

        def unit(s, v):
            if s is s0:
                half, part = divmod(v, HID0 // P)
                return (slice(HID0 + part * P, HID0 + part * P + P), slice(part * P, part * P + P),
                        slice(2 * HID0 + part * P, 2 * HID0 + part * P + P), half)
            half, part = divmod(v, ROW_GROUPS)
            at = ROW_GROUPS * P + part * P
            return slice(part * P, part * P + P), None, slice(at, at + P), half

        def wait(eng, s, value):
            if not (isinstance(value, int) and value <= 0):
                eng.wait_ge(s, value)

        def known(j):
            return isinstance(j, int)

        block = stack.enter_context(nc.Block())

        @block.sync
        def _(sp):
            sp.wait_ge(zeroed, 1)
            by_b = shifted[:, 0:NT, :].rearrange("p (b n) d -> p b n d", b=B)
            last = UNITS - NCONV - P
            first = T - UNITS - C - P
            x_by_row = x.rearrange("b t d -> t b d")
            for dst, start, n in ((shifted[0:CONV_ROWS, NT:NT + B, :], UNITS, CONV_ROWS),
                                  (by_b[:, :, 0, :], NCONV, P),
                                  (by_b[0:last, :, 1, :], NCONV + P, last),
                                  (by_b[:, :, 2, :], UNITS + C, P),
                                  (by_b[0:first, :, 3, :], UNITS + C + P, first)):
                sp.dma_start(dst, x_by_row[start:start + n, :, :]).then_inc(shift_loaded, 16)
            sp.dma_start(resid[:, :, :], x.rearrange("b t d -> (b t) d").rearrange("(n p) d -> p n d", p=P))\
                .then_inc(x_loaded, 16)
            sp.dma_start(conv_w_sb[:, :, :], conv_w.rearrange("r f o -> f r o")).then_inc(conv_loaded, 16)
            sp.wait_ge(zeroed, 2)
            by_b = addend[:, :, :].rearrange("p (b n) d -> p b n d", b=B)
            sp.dma_start(by_b[UNITS - NCONV - P:P, :, 1, :],
                         conv_b.unsqueeze(0).unsqueeze(0).broadcast_to([NCONV, B, P])).then_inc(add_loaded, 16)
            sp.dma_start(by_b[T - C - 3 * P:P, :, 3, :], ctx.rearrange("b c d -> c b d")).then_inc(add_loaded, 16)

            def load(s, src, sel_src, cols, n_sel):
                def body(j):
                    for slot in range(2):
                        r = j * 2 + slot
                        batches = s.per // s.batch
                        wait(sp, s.down_split, j * 4 + 2 * (slot - 1))
                        wait(sp, s.c_ready, j * (2 * batches) + batches * (slot - 1))
                        if s is s1 and known(j):
                            sp.wait_ge(s0.c_ready, s0.units // s0.batch)
                            sp.wait_ge(s0.down_split, 2 * s0.rounds)
                        sp.dma_start(raw[slot][:, 0:cols], src[r, :, :]).then_inc(s.loaded[slot], 16)
                        sp.dma_start(sel[slot][0:n_sel, :], sel_src[r, :, :]).then_inc(s.loaded[slot], 16)
                s.run(sp, body, 2)

            load(s0, w0_in, sel0_in.bitcast(BF16), 3 * HID0, 3 * E0)
            load(s1, w1_in, sel1_in.bitcast(BF16), 2 * ROW_GROUPS * P, P)
            for half in range(2):
                sp.wait_ge(out_ready, half + 1)
                n = NT // 2
                sp.dma_start(out.rearrange("b t d -> (b t) d").rearrange("(n p) d -> p n d", p=P)[:, half * n:half * n + n, :],
                             resid[:, half * n:half * n + n, :]).then_inc(stored, 16)
            sp.wait_ge(stored, 32)

        @block.gpsimd
        def _(pool):
            steps = [0]

            def step(ins):
                steps[0] += 1
                ins.then_inc(pool_step, 1)
                pool.wait_ge(pool_step, steps[0])

            pool.memset(shifted[:, :, :], 0.0).then_inc(zeroed, 1)
            pool.memset(addend[:, :, :], 0.0).then_inc(zeroed, 1)
            pool.memset(conv_x[:, :, :, :], 0.0).then_inc(zeroed, 1)
            pool.memset(nmax_pad[:, :, :], 0.0).then_inc(zeroed, 1)
            pool.memset(v_ones[:, :, :, :], 0.0).then_inc(zeroed, 1)
            pool.wait_ge(zeroed, 5)
            pool.memset(v_ones[:, :, :, D:D + 1], 1.0).then_inc(zeroed, 1)
            pool.wait_ge(par_loaded, 16)
            pool.wait_ge(par_hi_ready, 1)
            pool.tensor_tensor(par_lo[:, :], par[:, :], par_hi[:, :].bitcast(F32), ALU.subtract).then_inc(par_lo_ready, 1)
            pool.wait_ge(const_loaded, 16)
            pool.tensor_copy(ident_bf[:, :], ident).then_inc(ident_cast, 1)
            pool.memset(parts1[:, :, :, :], 0.0).then_inc(zeroed, 1)
            pool.wait_ge(zeroed, 7)

            def split_part(slot, cols, done, count):
                pool.tensor_tensor(w_hi[slot][:, cols], raw[slot][:, cols],
                                   const[:, ONES:ONES + 1].broadcast_to([P, cols.stop - cols.start]), ALU.mult)\
                    .then_inc(done, 1)
                pool.wait_ge(done, count + 1)
                pool.tensor_tensor(w_lo[slot][:, cols], raw[slot][:, cols], w_hi[slot][:, cols].bitcast(F32),
                                   ALU.subtract).then_inc(done, 1)
                pool.wait_ge(done, count + 2)

            def split(s, up, down, between=None):
                def body(j):
                    for i in range(s.body):
                        slot = i % 2
                        r = j * s.body + i
                        if s is s1 and known(j) and i == 2:
                            between()
                        pool.wait_ge(s.loaded[slot], j * (16 * s.body) + (i // 2) * 32 + 32)
                        wait(pool, s.up_read, (r - 1) * s.per)
                        if s is s1 and known(j) and i < 2:
                            pool.wait_ge(s0.down, s0.units)
                        split_part(slot, slice(0, up), s.up_split, r * 2)
                        wait(pool, s.down, (r - 1) * s.per)
                        split_part(slot, slice(up, down), s.down_split, r * 2)
                s.run(pool, body)

            def stack_keys():
                pool.wait_ge(k3_ready, GROUPS)
                step(pool.tensor_copy(k3_part[:, :, :, :], k3[:, :, :, :]))
                low = slice(2 * HG * D, STACK)
                step(pool.tensor_tensor(k3_part[low, :, :, :], k3[low, :, :, :], k3_part[low, :, :, :].bitcast(F32),
                                        ALU.subtract))
                for b in range(B):
                    for g in range(GROUPS):
                        step(pool.tensor_tensor(
                            k_stack[0:STACK, b, g * HG:(g + 1) * HG, :],
                            k3_part[:, g, b, :].bitcast(F32).unsqueeze(1).broadcast_to([STACK, HG, C]),
                            const[0:STACK, HMASK:HMASK + HG].unsqueeze(2).broadcast_to([STACK, HG, C]), ALU.mult))
                    pool.tensor_copy(k_stack[STACK:P, b, :, :],
                                     const[STACK:P, HSEL:HSEL + H].unsqueeze(2).broadcast_to([P - STACK, H, C]))\
                        .then_inc(k_stack_ready, 1)
                    pool.wait_ge(k_stack_ready, b + 1)

            def shared_low():
                for half in range(2):
                    c = slice(half * HALF, (half + 1) * HALF)
                    pool.wait_ge(shared_hi, half + 1)
                    pool.tensor_tensor(oT_lo[:, c], hw[:, half, :], oT_hi[:, c].bitcast(F32), ALU.subtract)\
                        .then_inc(shared_lo, 1)
                    pool.wait_ge(shared_lo, half + 1)

            split(s0, 2 * HID0, 3 * HID0)
            stack_keys()
            split(s1, ROW_GROUPS * P, 2 * ROW_GROUPS * P, shared_low)

        @block.scalar
        def _(act):
            act.dma_start(par[:, :], split_in).then_inc(par_loaded, 16)
            act.dma_start(const[:, :], consts_in).then_inc(const_loaded, 16)
            act.dma_start(bqk[:, :], bqk_in).then_inc(rows_loaded, 16)
            act.dma_start(rows[:, :], rows_in.broadcast_to([P, NROWS])).then_inc(rows_loaded, 16)

            def ln_std(n, tiles):
                act.preload_act_table(ACT.Sqrt)
                act.wait_ge(var_ready, n + 1)
                act.activation(std[:, 0:tiles, :], mv[:, 0:tiles, 1:2], ACT.Sqrt, bias=eps[:, :]).then_inc(std_ready, 1)

            def high_halves(n):
                for half in range(2):
                    act.wait_ge(xT_psum, 2 * n + half + 1)
                    act.activation(xT_hi[:, half * HALF:(half + 1) * HALF], bank[half], ACT.Copy)\
                        .then_inc(xT_hi_ready, 1)

            act.wait_ge(par_loaded, 16)
            act.activation(par_hi[:, :], par[:, :], ACT.Copy).then_inc(par_hi_ready, 1)
            act.wait_ge(eps_set, 1)
            ln_std(0, NT + B)
            ln_std(1, NT)
            high_halves(0)
            act.wait_ge(rows_loaded, 32)
            for g in range(GROUPS):
                act.wait_ge(k_psum, g // 2 * 2 + 2)
                act.activation(k3[:, g, :, :], bank[2 + g // 2][0:STACK, (g % 2) * B * C:(g % 2 + 1) * B * C]
                               .rearrange("p (b c) -> p b c", b=B),
                               ACT.Identity, bias=bqk[:, GROUPS + g:GROUPS + g + 1]).then_inc(k3_ready, 1)
            act.preload_act_table(ACT.Exp)
            act.wait_ge(diff_ready, 1)
            act.activation(top0[:, 3, :], top0[:, 2, :], ACT.Exp).then_inc(exp_ready, 1)

            def stream(s):
                def silu(u, v):
                    wait(act, s.b_ready, u + v + 1)
                    wait(act, s.gated if s.two_gates else s.hw, u + v - 1)
                    act.activation(silu_out[:, v % 2, :], bank[(2 if s.two_gates else 0) + v % 2], ACT.Silu)\
                        .then_inc(s.silu, 1)

                def high(u, v):
                    wait(act, s.hw, u + v + 1)
                    wait(act, s.down, u + v + 1 - NH)
                    act.activation(h_hi[v % NH][:, :], hw[:, v % 2, :], ACT.Copy).then_inc(s.hi, 1)

                def body(j):
                    u = j * (s.body * s.per)
                    for v in range(s.body * s.per):
                        silu(u, v)
                        if not (known(j) and v == 0):
                            high(u, v - 1)
                s.run(act, body)
                high(s.units, -1)
                act.wait_ge(*s.complete)
                act.activation(yT[:, 0:HALF], acc[0], ACT.Copy).then_inc(yT_ready[0], 1)

            stream(s0)
            ln_std(2, NT)
            high_halves(1)
            for i in range(B * GROUPS):
                b, g = divmod(i, GROUPS)
                act.wait_ge(q_psum, i + 1)
                act.activation(q_stack[0:STACK, g, b * T:(b + 1) * T], bank[2 + i % 4][0:STACK, :], ACT.Identity,
                               bias=bqk[:, g:g + 1]).then_inc(q_hi_ready, 1)

            def maxima(b):
                act.wait_ge(nmaxT_psum, (b + 1) * NT // B)
                for g in range(GROUPS):
                    act.activation(q_stack[STACK:P, g, b * T:(b + 1) * T], bank[b][STACK:P, :], ACT.Copy)\
                        .then_inc(q_max_ready[b], 1)

            maxima(0)
            act.preload_act_table(ACT.Exp)
            for i in range(B * H):
                if i == 2:
                    maxima(1)
                act.wait_ge(scoresT_ready, i + 1)
                wait(act, pv_done, i // HG - 1)
                act.activation(exps[:, i % NE, :], bank[(0, 2, 3)[i % 3]][0:C, :], ACT.Exp, scale=SCALE).then_inc(exp_done, 1)
            for b in range(B):
                act.wait_ge(oT_psum, b + 1)
                act.activation(oT_hi[:, b * T:(b + 1) * T], bank[b], ACT.Copy).then_inc(oT_hi_ready, 1)
            ln_std(3, NT)
            high_halves(2)
            act.preload_act_table(ACT.Sigmoid)
            act.wait_ge(lg1_ready, 1)
            act.activation(prob1, lg1, ACT.Sigmoid).then_inc(prob_ready, 1)
            for half in range(2):
                act.wait_ge(shared_gate, half + 1)
                act.activation(hw[:, half, :], bank[5 + 2 * half], ACT.Silu).then_inc(shared_silu, 1)
                act.wait_ge(shared_silu, half + 1)
                act.activation(oT_hi[:, half * HALF:(half + 1) * HALF], hw[:, half, :], ACT.Copy).then_inc(shared_hi, 1)
            for k in (0, 1):
                act.wait_ge(combT1_psum, k + 1)
                act.activation(combT1[:, k, :], bank[2 + k].bitcast(BF16), ACT.Copy).then_inc(combT1_ready, 1)
            stream(s1)

        @block.vector
        def _(dve):
            steps = [0]

            def step(ins):
                steps[0] += 1
                ins.then_inc(dve_step, 1)
                dve.wait_ge(dve_step, steps[0])

            def layer_norm(n, src, tiles):
                last = None
                for t in range(tiles):
                    last = dve.bn_stats(stats[:, t, :], src[:, t, :])
                step(last)
                for t in range(tiles):
                    last = dve.bn_aggr(mv[:, t, :], stats[:, t, :])
                last.then_inc(var_ready, 1)
                dve.wait_ge(std_ready, n + 1)
                step(dve.reciprocal(rstd[:, 0:tiles, :], std[:, 0:tiles, :]))
                order = list(range(NT, tiles)) + list(range(min(tiles, NT)))
                for t in order:
                    dve.tensor_scalar(xn[:, t, :], src[:, t, :], mv[:, t, 0:1], rstd[:, t, :], ALU.subtract, ALU.mult)\
                        .then_inc(xn_ready, 1)

            def low_halves(n):
                for half in range(2):
                    cols = slice(half * HALF, (half + 1) * HALF)
                    dve.wait_ge(xT_hi_ready, 2 * n + half + 1)
                    dve.tensor_tensor(xT_lo[:, cols], bank[half], xT_hi[:, cols].bitcast(F32), ALU.subtract)\
                        .then_inc(xT_lo_ready, 1)

            dve.memset(eps[:, :], EPS).then_inc(eps_set, 1)
            dve.wait_ge(shift_loaded, 16 * 5)
            layer_norm(0, shifted, NT + B)
            dve.wait_ge(convT_psum, 1)
            dve.wait_ge(zeroed, 3)
            at = UNITS - NCONV - P
            dve.tensor_copy(conv_x[:, :, :, at:P],
                            bank[0][:, 0:B * P].rearrange("p (b m) -> p b m", b=B)[:, :, 0:CONV_ROWS]
                            .rearrange("p b (j r) -> p b r j", r=RATE)).then_inc(conv_x_ready, 1)
            dve.wait_ge(x_loaded, 16)
            dve.wait_ge(xn_ready, NT + B)
            step(dve.tensor_tensor(resid[:, :, :], resid[:, :, :], xn[:, 0:NT, :], ALU.add))
            dve.wait_ge(add_loaded, 16 * 2)
            odd = resid[:, :, :].rearrange("p (n two) d -> p n two d", two=2)[:, :, 1, :]
            step(dve.tensor_tensor(odd, odd, addend[:, :, :].rearrange("p (n two) d -> p n two d", two=2)[:, :, 1, :],
                                   ALU.add))
            dve.wait_ge(conv_done, 1)
            conv_tiles = resid[:, :, :].rearrange("p (b n) d -> p b n d", b=B)[:, :, 1, :]
            step(dve.tensor_tensor(conv_tiles, conv_tiles, bank[1][:, 0:B * P].rearrange("p (b d) -> p b d", b=B),
                                   ALU.add))

            layer_norm(1, resid, NT)
            low_halves(0)
            dve.wait_ge(v_psum, 1)
            dve.wait_ge(zeroed, 6)
            dve.wait_ge(rows_loaded, 32)
            for b in range(B):
                dve.tensor_tensor(v_ones[:, b, :, 0:D],
                                  bank[4][0:C, b * P:(b + 1) * P].rearrange("p (h d) -> p h d", h=H),
                                  rows[0:C, BV:BV + P].rearrange("p (h d) -> p h d", h=H), ALU.add).then_inc(v_ready, 1)
            dve.wait_ge(logits0, 1)
            step(dve.tensor_tensor(lg0[:, :, :], bank[5][:, 0:NT * E0].rearrange("p (n e) -> p n e", n=NT),
                                   rows[:, RB0:RB0 + E0].unsqueeze(1).broadcast_to([P, NT, E0]), ALU.add))
            other = lg0[:, :, :].unsqueeze(2).broadcast_to([P, NT, E0, E0])
            own = lg0[:, :, :].unsqueeze(3).broadcast_to([P, NT, E0, E0])
            dve.tensor_tensor(pair_gt[:, :, :, :], other, own, ALU.is_gt)
            step(dve.tensor_tensor(pair_eq[:, :, :, :], other, own, ALU.is_equal))
            flat = "p n a b -> p n (a b)"
            dve.wait_ge(const_loaded, 16)
            step(dve.tensor_tensor(pair_eq[:, :, :, :].rearrange(flat), pair_eq[:, :, :, :].rearrange(flat),
                                   const[:, TRI:TRI + E0 * E0].unsqueeze(1).broadcast_to([P, NT, E0 * E0]), ALU.mult))
            step(dve.tensor_tensor(pair_gt[:, :, :, :], pair_gt[:, :, :, :], pair_eq[:, :, :, :], ALU.add))
            step(dve.tensor_reduce(rank0[:, :, :], pair_gt[:, :, :, :], AX.X, ALU.add))
            dve.tensor_scalar(chosen0[:, :, :], rank0[:, :, :], 2.0, None, ALU.is_lt).then_inc(chosen_ready, 1)
            dve.tensor_scalar(second0[:, :, :], rank0[:, :, :], 1.0, None, ALU.is_equal)
            dve.tensor_scalar(first0[:, :, :], rank0[:, :, :], 0.0, None, ALU.is_equal)
            step(dve.tensor_reduce(top0[:, 0, :], lg0[:, :, :], AX.X, ALU.max))
            step(dve.tensor_tensor(tmp0[:, :, :], lg0[:, :, :], second0[:, :, :], ALU.mult))
            step(dve.tensor_reduce(top0[:, 1, :], tmp0[:, :, :], AX.X, ALU.add))
            dve.tensor_tensor(top0[:, 2, :], top0[:, 1, :], top0[:, 0, :], ALU.subtract).then_inc(diff_ready, 1)
            dve.wait_ge(exp_ready, 1)
            step(dve.tensor_scalar(top0[:, 4, :], top0[:, 3, :], 1.0, None, ALU.add))
            step(dve.reciprocal(top0[:, 4, :], top0[:, 4, :]))
            step(dve.tensor_tensor(top0[:, 5, :], top0[:, 3, :], top0[:, 4, :], ALU.mult))
            dve.tensor_tensor(first0[:, :, :], first0[:, :, :],
                              top0[:, 4, :].unsqueeze(2).broadcast_to([P, NT, E0]), ALU.mult)
            step(dve.tensor_tensor(second0[:, :, :], second0[:, :, :],
                                   top0[:, 5, :].unsqueeze(2).broadcast_to([P, NT, E0]), ALU.mult))
            step(dve.tensor_tensor(comb0[:, :, :], first0[:, :, :], second0[:, :, :], ALU.add))
            dve.wait_ge(place_ready, 1)
            step(dve.scalar_tensor_tensor(comb0[:, :, :], bank[4][:, 256:256 + NT * E0].rearrange("p (n e) -> p n e", n=NT),
                                          float(CAPACITY), comb0[:, :, :], ALU.is_lt, ALU.mult))
            rest = tmp0[:, :, :]
            step(dve.tensor_copy(parts0[:, :, 0, :], comb0[:, :, :]))
            step(dve.tensor_tensor(rest, comb0[:, :, :], parts0[:, :, 0, :], ALU.subtract))
            step(dve.tensor_copy(parts0[:, :, 1, :], rest))
            dve.tensor_tensor(parts0[:, :, 2, :], rest, parts0[:, :, 1, :], ALU.subtract).then_inc(parts0_ready, 1)
            dve.wait_ge(combT0_psum, 1)
            dve.tensor_copy(combT0[:, :], bank[6].bitcast(BF16)[0:3 * E0, :]).then_inc(combT0_ready, 1)

            def stream(s):
                def multiply(u, c, v):
                    i = v % 2
                    wait(dve, s.silu, u + v + 1)
                    src = silu_out[:, i, :]
                    if s.two_gates:
                        wait(dve, s.a_ready, u + v + 1)
                        dve.tensor_tensor(gated[:, i, :], src, bank[i], ALU.mult).then_inc(s.gated, 1)
                        wait(dve, s.gated, u + v + 1)
                        src = gated[:, i, :]
                        weights = bank[4 + v // s.batch % 2]
                    else:
                        weights = bank[2 + v % ROW_GROUPS]
                    wait(dve, s.c_ready, c + v // s.batch + 1)
                    wait(dve, s.hi, u + v - 1)
                    wait(dve, s.lo, u + v - 1)
                    dve.tensor_tensor(hw[:, i, :], src, weights, ALU.mult).then_inc(s.hw, 1)

                def low(u, v):
                    wait(dve, s.hi, u + v + 1)
                    dve.tensor_tensor(h_lo[v % NH][:, :], hw[:, v % 2, :], h_hi[v % NH][:, :].bitcast(F32),
                                      ALU.subtract).then_inc(s.lo, 1)

                def body(j):
                    u, c = j * (s.body * s.per), j * (s.body * s.per // s.batch)
                    for v in range(s.body * s.per):
                        multiply(u, c, v)
                        if not (known(j) and v == 0):
                            low(u, v - 1)
                s.run(dve, body)
                low(s.units, -1)
                dve.wait_ge(*s.complete)
                dve.tensor_copy(yT[:, HALF:2 * HALF], acc[1]).then_inc(yT_ready[1], 1)

            def add_back(n, ready):
                for half in range(2):
                    part = resid[:, half * NT // 2:(half + 1) * NT // 2, :]
                    dve.wait_ge(y_psum, 2 * n + half + 1)
                    ready(dve.tensor_tensor(part, part, bank[half].rearrange("p (n d) -> p n d", d=P), ALU.add))

            stream(s0)
            add_back(0, step)

            layer_norm(2, resid, NT)
            low_halves(1)
            mid = slice(HG * D, 2 * HG * D)
            for i in range(B * GROUPS):
                b, g = divmod(i, GROUPS)
                dve.wait_ge(q_hi_ready, i + 1)
                dst = q_stack[mid, g, b * T:(b + 1) * T]
                dve.scalar_tensor_tensor(dst, bank[2 + i % 4][mid, :], bqk[mid, g:g + 1], dst.bitcast(F32),
                                         ALU.add, ALU.subtract).then_inc(q_lo_ready, 1)
            for t in range(NT):
                for pair in range(2):
                    n = 2 * t + pair
                    at = 2 + 2 * (n % 3)
                    dve.wait_ge(scores_ready, n + 1)
                    dve.tensor_reduce(nmax[:, t, 2 * pair * HG:2 * (pair + 1) * HG].rearrange("p (k h) -> p k h", k=2),
                                      psum[:, at:at + 2, 0:HG * C].rearrange("p k (h c) -> p k h c", h=HG),
                                      AX.X, ALU.max, negate=True).then_inc(max_taken, 1)
                dve.wait_ge(max_taken, 2 * t + 2)
                wait(dve, nmaxT_psum, t - 1)
                dst = nmax_pad[:, t % 2, STACK:STACK + H]
                step(dve.tensor_copy(dst.bitcast(F32R), nmax[:, t, :]))
                dve.tensor_tensor(nmax_pad[:, t % 2, STACK + H:P].bitcast(F32R), nmax[:, t, :], dst, ALU.subtract)\
                    .then_inc(nmax_ready, 1)
            step(dve.tensor_tensor(resid[:, :, :], resid[:, :, :],
                                   rows[:, BO:BO + P].unsqueeze(1).broadcast_to([P, NT, P]), ALU.add))

            def copy_group(n):
                dve.wait_ge(pv_done, n + 1)
                wait(dve, pv_turned, n - 1)
                dve.tensor_copy(pv_sb[:, n % 2, :], bank[4 + n % 4]).then_inc(pv_copied, 1)

            def normalise_group(n):
                b, g = divmod(n, GROUPS)
                t0 = b * (NT // B)
                dve.wait_ge(pv_turned, n + 1)
                pv = bank[1].rearrange("p (t h d) -> p t h d", t=NT // B, h=HG)
                step(dve.reciprocal(inv[:, n % 2, :, :], pv[:, :, :, D]))
                dve.tensor_tensor(onat[:, t0:t0 + NT // B, g * HG * D:(g + 1) * HG * D].rearrange("p t (h d) -> p t h d", h=HG),
                                  pv[:, :, :, 0:D],
                                  inv[:, n % 2, :, :].unsqueeze(3).broadcast_to([P, NT // B, HG, D]), ALU.mult)\
                    .then_inc(onat_ready, 1)

            for n in range(B * GROUPS):
                copy_group(n)
                if n >= 1:
                    normalise_group(n - 1)
            normalise_group(B * GROUPS - 1)
            for b in range(B):
                cols = slice(b * T, (b + 1) * T)
                dve.wait_ge(oT_hi_ready, b + 1)
                dve.tensor_tensor(oT_lo[:, cols], bank[b], oT_hi[:, cols].bitcast(F32), ALU.subtract)\
                    .then_inc(oT_lo_ready, 1)
            for b in range(B):
                part = resid[:, b * NT // B:(b + 1) * NT // B, :]
                dve.wait_ge(proj_done, b + 1)
                step(dve.tensor_tensor(part, part, bank[2 + b].rearrange("p (n d) -> p n d", d=P), ALU.add))

            layer_norm(3, resid, NT)
            low_halves(2)
            for k, (t0, t1) in enumerate(((0, 3), (3, 6), (6, 8))):
                dve.wait_ge(logits1, k + 1)
                last = dve.tensor_tensor(lg1[:, t0:t1, :], bank[2 + k][:, 0:(t1 - t0) * E1].rearrange("p (n e) -> p n e", e=E1),
                                         rows[:, EB:EB + E1].unsqueeze(1).broadcast_to([P, t1 - t0, E1]), ALU.add)
            last.then_inc(lg1_ready, 1)
            dve.wait_ge(lg1_ready, 1)
            step(dve.tensor_scalar(key1, lg1, SIG_LOW, SIG_HIGH, ALU.max, ALU.min))
            for t in range(NT):
                last = dve.max(best1[:, t, :], key1[:, t, :])
            step(last)
            for t in range(NT):
                last = dve.match_replace(key1[:, t, :], best1[:, t, :], key1[:, t, :], -3e38)
            step(last)
            dve.wait_ge(prob_ready, 1)
            for t in range(NT):
                last = dve.scalar_tensor_tensor(comb1[:, t, :], key1[:, t, :], -1e38, prob1[:, t, :],
                                                ALU.is_lt, ALU.mult, accum_out=sum1[:, t:t + 1])
            step(last)
            step(dve.tensor_scalar(sum1[:, :], sum1[:, :], 1e-9, None, ALU.add))
            step(dve.reciprocal(sum1[:, :], sum1[:, :]))
            step(dve.tensor_scalar(sum1[:, :], sum1[:, :], ROUTED_SCALE, None, ALU.mult))
            cell = parts1[:, :, :, :]
            dve.wait_ge(zeroed, 7)
            by_cell = "p (c e) -> p c e"
            for t in range(NT):
                last = dve.tensor_scalar(cell[:, t, :, 0:EC], comb1[:, t, :].rearrange(by_cell, e=EC), sum1[:, t:t + 1],
                                         None, ALU.mult)
            step(last)
            for t in range(NT):
                last = dve.scalar_tensor_tensor(lg1[:, t, :].rearrange(by_cell, e=EC), comb1[:, t, :].rearrange(by_cell, e=EC),
                                                sum1[:, t:t + 1], cell[:, t, :, 0:EC], ALU.mult, ALU.subtract)
            step(last)
            all_cells = cell.rearrange("p n c r -> p (n c) r")
            left = lg1.rearrange("p n (c e) -> p (n c) e", e=EC)
            step(dve.tensor_copy(all_cells[:, :, EC:2 * EC], left))
            dve.tensor_tensor(all_cells[:, :, 2 * EC:3 * EC], left, all_cells[:, :, EC:2 * EC], ALU.subtract)\
                .then_inc(parts1_ready, 1)
            for k in (2, 3):
                dve.wait_ge(combT1_psum, k + 1)
                dve.tensor_copy(combT1[:, k, :], bank[2 + k].bitcast(BF16)).then_inc(combT1_ready, 1)
            stream(s1)
            add_back(1, lambda ins: ins.then_inc(out_ready, 1))

        @block.tensor
        def _(pe):
            mm = nc.tensor.matmul

            def three(dst, w, rhs, start, stop):
                (wh, wl), (rh, rl) = w, rhs
                mm(dst, wh, rh, start=start, stop=False)
                mm(dst, wh, rl, start=False, stop=False)
                return mm(dst, wl, rh, start=False, stop=stop)

            def cols(half):
                c = slice(half * HALF, (half + 1) * HALF)
                return xT_hi[:, c], xT_lo[:, c]

            def tile_of(t):
                c = slice(t * P, (t + 1) * P)
                return xT_hi[:, c], xT_lo[:, c]

            def transpose_rows(before):
                for t in range(NT):
                    pe.wait_ge(xn_ready, before + t + 1)
                    last = nc.tensor.transpose(bank[t // 4][:, (t % 4) * P:(t % 4 + 1) * P], xn[:, t, :], ident)
                    if t % 4 == 3:
                        last.then_inc(xT_psum, 1)

            pe.wait_ge(par_hi_ready, 1)
            pe.wait_ge(par_lo_ready, 1)
            for g in range(GROUPS):
                c = (g * STACK, (g + 1) * STACK)
                three(bank[2 + g // 2][0:STACK, (g % 2) * B * C:(g % 2 + 1) * B * C],
                      (hi("wk", *c), lo("wk", *c)), (hi("ctxT"), lo("ctxT")), True, True).then_inc(k_psum, 1)
            for b in range(B):
                c = (b * C, (b + 1) * C)
                last = three(bank[4][0:C, b * P:(b + 1) * P], (hi("ctxT", *c), lo("ctxT", *c)), (hi("wv"), lo("wv")),
                             True, True)
            last.then_inc(v_psum, 1)
            pe.wait_ge(const_loaded, 16)
            for b in range(B):
                pe.wait_ge(xn_ready, b + 1)
                last = nc.tensor.transpose(bank[0][:, b * P:(b + 1) * P], xn[:, NT + b, :], ident)
            last.then_inc(convT_psum, 1)
            pe.wait_ge(conv_x_ready, 1)
            pe.wait_ge(conv_loaded, 16)
            for b in range(B):
                for r in range(RATE):
                    last = mm(bank[1][:, b * P:(b + 1) * P], conv_x[:, b, r, :], conv_w_sb[:, r, :],
                              start=r == 0, stop=r == RATE - 1)
            last.then_inc(conv_done, 1)

            transpose_rows(NT + B)
            for t in range(NT):
                pe.wait_ge(xT_lo_ready, t // 4 + 1)
                last = three(bank[5][:, t * E0:(t + 1) * E0], tile_of(t), (hi("rw0"), lo("rw0")), True, True)
            last.then_inc(logits0, 1)
            pe.wait_ge(chosen_ready, 1)
            pe.wait_ge(v_ready, B)
            place = bank[4][:, 256:256 + NT * E0]
            picks = chosen0[:, :, :].rearrange("p n e -> p (n e)")
            mm(place, const[:, ULT:ULT + P], picks, start=True, stop=False)
            for d in range(1, NT):
                last = mm(place[:, d * E0:], const[:, ONES:ONES + P], picks[:, 0:(NT - d) * E0], start=False,
                          stop=d == NT - 1)
            last.then_inc(place_ready, 1)

            def turn_comb0():
                pe.wait_ge(parts0_ready, 1)
                pe.wait_ge(ident_cast, 1)
                for t in range(NT):
                    last = nc.tensor.transpose(bank[6].bitcast(BF16)[0:3 * E0, t * P:(t + 1) * P],
                                               parts0[:, t, :, :].rearrange("p j e -> p (j e)"), ident_bf[:, :])
                last.then_inc(combT0_psum, 1)
                pe.wait_ge(combT0_ready, 1)

            def stream(s, before_combine=None):
                def up(j, u, v):
                    i, r = v // s.per, v % 2
                    slot = i % 2
                    gate, lin, _, half = unit(s, v % s.per)
                    if v % s.per == 0:
                        pe.wait_ge(s.up_split, j * (2 * s.body) + 2 * i + 2)
                    wait(pe, s.silu, u + v - 1)
                    three(bank[(2 if s.two_gates else 0) + r], (w_hi[slot][:, gate], w_lo[slot][:, gate]), cols(half),
                          True, True).then_inc(s.b_ready, 1)
                    if s.two_gates:
                        wait(pe, s.gated, u + v - 1)
                        three(bank[r], (w_hi[slot][:, lin], w_lo[slot][:, lin]), cols(half), True, True)\
                            .then_inc(s.a_ready, 1)

                def combine(j, u, v):
                    i = v // s.per
                    slot = i % 2
                    _, _, _, half = unit(s, v % s.per)
                    c = slice(half * HALF, (half + 1) * HALF)
                    if v % s.per == 0:
                        pe.wait_ge(s.loaded[slot], j * (16 * s.body) + (i // 2) * 32 + 32)
                    wait(pe, s.hw, u + v - s.batch)
                    if s.two_gates:
                        mm(bank[4 + v // s.batch % 2], sel[slot][0:3 * E0, :], combT0[:, c], start=True, stop=True)\
                            .then_inc(s.c_ready, 1)
                        return
                    for g in range(v % ROW_GROUPS, v % ROW_GROUPS + s.batch):
                        k = slice(g * CELL, g * CELL + 3 * EC)
                        last = mm(bank[2 + g], sel[slot][k, :], combT1[k, i, c], start=True, stop=True)
                    last.then_inc(s.c_ready, 1)

                def down(j, u, v, first=False, last=False):
                    slot = (v // s.per) % 2
                    _, _, cols_down, half = unit(s, v % s.per)
                    if v % s.per == 0:
                        pe.wait_ge(s.down_split, j * (2 * s.body) + 2 * (v // s.per) + 2)
                    wait(pe, s.lo, u + v + 1)
                    three(acc[half], (w_hi[slot][:, cols_down], w_lo[slot][:, cols_down]),
                          (h_hi[v % NH][:, :], h_lo[v % NH][:, :]), first, last).then_inc(s.down, 1)

                def body(j):
                    u = j * (s.body * s.per)
                    for v in range(s.body * s.per):
                        up(j, u, v)
                        if known(j) and v == 1 and before_combine:
                            before_combine()
                        if s.two_gates:
                            if known(j) and v == 1:
                                combine(j, u, 0)
                            elif v % s.batch == 0 and not (known(j) and v == 0):
                                combine(j, u, v)
                        if not known(j) or v >= s.lag:
                            down(j, u, v - s.lag, first=known(j) and v - s.lag in (0, s.per // 2))
                        if not s.two_gates and v % s.batch == 0:
                            combine(j, u, v)
                s.run(pe, body)
                for v in range(-s.lag, 0):
                    down(s.rounds // s.body, s.units, v, last=s is s0 and v in (-1, -1 - s.per // 2))

            def transpose_back(n):
                for t in range(NT):
                    pe.wait_ge(yT_ready[t // 4], n + 1)
                    last = nc.tensor.transpose(bank[t // 4][:, (t % 4) * P:(t % 4 + 1) * P], yT[:, t * P:(t + 1) * P],
                                               ident)
                    if t % 4 == 3:
                        last.then_inc(y_psum, 1)

            pe.wait_ge(k3_ready, GROUPS)
            stream(s0, turn_comb0)
            transpose_back(0)

            transpose_rows(2 * NT + B)
            for i in range(B * GROUPS):
                b, g = divmod(i, GROUPS)
                c = (g * STACK, (g + 1) * STACK)
                pe.wait_ge(xT_lo_ready, 2 + b + 1)
                wait(pe, q_lo_ready, i - 3)
                three(bank[2 + i % 4][0:STACK, :], (hi("wq", *c), lo("wq", *c)), cols(b), True, True).then_inc(q_psum, 1)
            pe.wait_ge(k_stack_ready, B)

            def turn_max(t):
                pe.wait_ge(nmax_ready, t + 1)
                nc.tensor.transpose(bank[t // 4][:, (t % 4) * P:(t % 4 + 1) * P], nmax_pad[:, t % 2, :], ident)\
                    .then_inc(nmaxT_psum, 1)

            pe.wait_ge(q_lo_ready, B * GROUPS)
            for t in range(NT):
                b = t // (NT // B)
                for pair in range(2):
                    n = 2 * t + pair
                    wait(pe, max_taken, n - 2)
                    for k in range(2):
                        g = 2 * pair + k
                        last = mm(bank[2 + 2 * (n % 3) + k][:, 0:HG * C], q_stack[0:STACK, g, t * P:(t + 1) * P],
                                  k_stack[0:STACK, b, g * HG:(g + 1) * HG, :].rearrange("p h c -> p (h c)"),
                                  start=True, stop=True)
                    last.then_inc(scores_ready, 1)
                if t >= 2:
                    turn_max(t - 2)
            turn_max(NT - 2)
            turn_max(NT - 1)

            def values(n):
                b, g = divmod(n, GROUPS)
                pe.wait_ge(exp_done, HG * (n + 1))
                wait(pe, pv_copied, n - 3)
                for j in range(HG):
                    last = mm(bank[4 + n % 4][CELL * j:CELL * (j + 1), :], v_ones[:, b, g * HG + j, :],
                              exps[:, (n * HG + j) % NE, :], start=True, stop=True)
                last.then_inc(pv_done, 1)

            def turn_group(n):
                pe.wait_ge(pv_copied, n + 1)
                pe.wait_ge(q_max_ready[1], GROUPS)
                wait(pe, onat_ready, n)
                for t in range(NT // B):
                    last = nc.tensor.transpose(bank[1][:, t * P:(t + 1) * P], pv_sb[:, n % 2, t * P:(t + 1) * P], ident)
                last.then_inc(pv_turned, 1)

            pe.wait_ge(max_taken, 2 * NT)
            for i in range(B * H):
                b, h = divmod(i, H)
                pe.wait_ge(q_max_ready[b], GROUPS)
                wait(pe, exp_done, i - 2)
                mm(bank[(0, 2, 3)[i % 3]][0:C, :], k_stack[:, b, h, :], q_stack[:, h // HG, b * T:(b + 1) * T],
                   start=True, stop=True).then_inc(scoresT_ready, 1)
                if i >= HG + 1 and (i - HG - 1) % HG == 0:
                    n = (i - HG - 1) // HG
                    values(n)
                    if n >= 1:
                        turn_group(n - 1)
            values(B * GROUPS - 1)
            turn_group(B * GROUPS - 2)
            turn_group(B * GROUPS - 1)
            for b in range(B):
                pe.wait_ge(onat_ready, (b + 1) * GROUPS)
                for t in range(NT // B):
                    last = nc.tensor.transpose(bank[b][:, t * P:(t + 1) * P], onat[:, b * (NT // B) + t, :], ident)
                last.then_inc(oT_psum, 1)
            for b in range(B):
                pe.wait_ge(oT_lo_ready, b + 1)
                for t in range(NT // B):
                    c = slice((b * (NT // B) + t) * P, (b * (NT // B) + t + 1) * P)
                    last = three(bank[2 + b][:, t * P:(t + 1) * P], (oT_hi[:, c], oT_lo[:, c]), (hi("wo"), lo("wo")),
                                 True, True)
                last.then_inc(proj_done, 1)

            transpose_rows(3 * NT + B)
            for k, (t0, t1) in enumerate(((0, 3), (3, 6), (6, 8))):
                for t in range(t0, t1):
                    pe.wait_ge(xT_lo_ready, 4 + t // 4 + 1)
                    last = three(bank[2 + k][:, (t - t0) * E1:(t - t0 + 1) * E1], tile_of(t), (hi("rw1"), lo("rw1")),
                                 True, True)
                last.then_inc(logits1, 1)
            for half in range(2):
                three(bank[5 + 2 * half], (hi("wgs"), lo("wgs")), cols(half), True, True).then_inc(shared_gate, 1)
            pe.wait_ge(lg1_ready, 1)
            pe.wait_ge(shared_silu, 2)
            pe.wait_ge(shared_lo, 2)
            pe.wait_ge(parts1_ready, 1)
            for k in range(KT):
                for t in range(NT):
                    last = nc.tensor.transpose(bank[2 + k].bitcast(BF16)[:, t * P:(t + 1) * P],
                                               parts1[:, t, k * ROW_GROUPS:(k + 1) * ROW_GROUPS, :]
                                               .rearrange("p c r -> p (c r)"), ident_bf[:, :])
                last.then_inc(combT1_psum, 1)
            pe.wait_ge(combT1_ready, KT)
            stream(s1)
            for half in range(2):
                c = slice(half * HALF, (half + 1) * HALF)
                last = three(acc[half], (hi("wds"), lo("wds")), (oT_hi[:, c], oT_lo[:, c]), False, True)
            last.then_inc(sum_done, 1)
            transpose_back(1)


def kernel(x, ctx_1024, L0_xattn_conv_w, L0_xattn_conv_b, L0_ffn_router_w, L0_ffn_router_b, L0_ffn_W, L0_ffn_V,
           L0_ffn_W_out, L1_xattn_Wq, L1_xattn_bq, L1_xattn_Wk, L1_xattn_bk, L1_xattn_Wv, L1_xattn_bv, L1_xattn_Wo,
           L1_xattn_bo, L1_ffn_router_w, L1_ffn_expert_bias, L1_ffn_w_gate, L1_ffn_w_down, L1_ffn_w_gate_shared,
           L1_ffn_w_down_shared):
    import numpy as np
    import concourse.bacc as bacc
    from concourse.bass_utils import run_bass_kernel_spmd

    def arr(a):
        return np.asarray(a)

    def stacked(w):
        g = arr(w).T.reshape(P, GROUPS, HG * D)
        return np.concatenate([g, g, g], axis=2).reshape(P, GROUPS * STACK)

    def stacked_bias(v):
        g = arr(v).reshape(GROUPS, HG * D).T
        return np.concatenate([g, g, g], axis=0)

    f32 = np.float32
    ctx = arr(ctx_1024)
    shared_gate = np.concatenate([arr(L1_ffn_w_gate_shared).T, np.zeros((P, P - INTER), f32)], axis=1)
    shared_down = np.concatenate([arr(L1_ffn_w_down_shared).T, np.zeros((P - INTER, P), f32)], axis=0)
    columns = {"rw0": arr(L0_ffn_router_w).T, "ctxT": ctx.reshape(B * C, P).T, "wk": stacked(L1_xattn_Wk),
               "wv": arr(L1_xattn_Wv).T, "wq": stacked(L1_xattn_Wq), "wo": arr(L1_xattn_Wo).T,
               "rw1": arr(L1_ffn_router_w).T, "wgs": shared_gate, "wds": shared_down}
    split_in = np.concatenate([columns[n] for n in SPLIT], axis=1)
    rows_in = np.concatenate([arr(L0_ffn_router_b), arr(L1_xattn_bv), arr(L1_xattn_bo), arr(L1_ffn_expert_bias)])[None, :]
    bqk_in = np.concatenate([stacked_bias(L1_xattn_bq), stacked_bias(L1_xattn_bk)], axis=1)
    w0_in = np.concatenate([arr(L0_ffn_W), arr(L0_ffn_V),
                            arr(L0_ffn_W_out).reshape(E0, HID0 // P, P, P).transpose(0, 2, 1, 3).reshape(E0, P, HID0)],
                           axis=2)
    gate = arr(L1_ffn_w_gate).reshape(KT, ROW_GROUPS, EC // 2, 2, INTER, P).transpose(2, 0, 5, 1, 3, 4)\
        .reshape(ROUNDS1, P, ROW_GROUPS * P)
    down = arr(L1_ffn_w_down).reshape(KT, ROW_GROUPS, EC // 2, 2, P, INTER).transpose(2, 0, 3, 5, 1, 4)\
        .reshape(ROUNDS1, P, ROW_GROUPS * P)
    w1_in = np.concatenate([gate, down], axis=2)

    consts_in = np.zeros((P, NCONST), f32)
    i = np.arange(P)
    consts_in[:, IDENT:IDENT + P] = np.eye(P, dtype=f32)
    consts_in[:, ULT:ULT + P] = i[:, None] < i[None, :]
    consts_in[:, ONES:ONES + P] = 1
    e = np.arange(E0)
    consts_in[:, TRI:TRI + E0 * E0] = (e[None, :] < e[:, None]).reshape(1, E0 * E0)
    for j in range(HG):
        consts_in[:, HMASK + j] = (i % (HG * D)) // D == j
    for h in range(H):
        consts_in[STACK + h, HSEL + h] = 1
        consts_in[STACK + H + h, HSEL + h] = 1
    one = 0x3F80
    sel0_in = np.zeros((E0, 3 * E0, P), np.uint16)
    for n in range(E0):
        sel0_in[n, n::E0, :] = one
    sel1_in = np.zeros((ROUNDS1, P, P), np.uint16)
    for r in range(ROUNDS1):
        for g in range(ROW_GROUPS):
            for part in range(3):
                row = g * CELL + part * EC + 2 * (r // KT)
                sel1_in[r, row, 0:INTER] = one
                sel1_in[r, row + 1, INTER:P] = one

    arrays = {"x": arr(x), "ctx": ctx, "conv_w": arr(L0_xattn_conv_w), "conv_b": arr(L0_xattn_conv_b),
              "split_in": split_in, "consts_in": consts_in, "rows_in": rows_in, "bqk_in": bqk_in, "w0_in": w0_in,
              "sel0_in": sel0_in, "w1_in": w1_in, "sel1_in": sel1_in}
    arrays = {n: np.ascontiguousarray(a) for n, a in arrays.items()}
    nc = bacc.Bacc("TRN2", target_bir_lowering=False, num_devices=1)
    args = [nc.dram_tensor(n, a.shape, mybir.dt.from_np(a.dtype), kind="ExternalInput").ap() for n, a in arrays.items()]
    out = nc.dram_tensor("out", (B, T, P), F32, kind="ExternalOutput").ap()
    build_program(nc, *args, out)
    result = run_bass_kernel_spmd(nc, [arrays], core_ids=[0])
    return result.results[0]["out"]
```

```python
import concourse.bass as bass
from concourse import mybir
from contextlib import ExitStack

F32 = mybir.dt.float32
F32R = mybir.dt.float32r
BF16 = mybir.dt.bfloat16
ALU = mybir.AluOpType
ACT = mybir.ActivationFunctionType
AX = mybir.AxisListType

P = 128
B, T, C = 2, 512, 77
NT = B * T // P
HALF = 512
EPS = 1e-5
UNITS, RATE = 256, 4
NCONV = (C - RATE) // RATE + 1
CONV_ROWS = NCONV * RATE
E0, HID0, CAPACITY = 8, 256, 256
H, D = 16, 8
GROUPS, HG = 4, 4
STACK = 3 * HG * D
SCALE = D ** -0.5
E1, INTER, TOP, ROUTED_SCALE = 160, 64, 8, 2.5
ROW_GROUPS, KT = 4, 4
EC = E1 // (ROW_GROUPS * KT)
CELL = 32
ROUNDS1 = E1 // (2 * ROW_GROUPS)
GATE_SETS = ((0, 3), (3, 6), (6, 8))
SIG_LOW, SIG_HIGH = -88.72, 17.33

SPLIT = {}
_at = 0
for _name, _n in (("rw0", E0), ("ctxT", B * C), ("wk", GROUPS * STACK), ("wv", P), ("wq", GROUPS * STACK),
                  ("wo", P), ("rw1", E1), ("wgs", P), ("wds", P)):
    SPLIT[_name] = (_at, _at + _n)
    _at += _n
NSPLIT = _at
IDENT, ULT, ONES, TRI, HMASK, HSEL = 0, P, 2 * P, 3 * P, 3 * P + 64, 3 * P + 68
NCONST = 3 * P + 84
RB0, BV, BO, EB = 0, E0, E0 + P, E0 + 2 * P
NROWS = E0 + 2 * P + E1


def build_program(nc, x, ctx, conv_w, conv_b, split_in, consts_in, rows_in, bqk_in, w0_in, sel0_in, w1_in, sel1_in, out):
    stack = ExitStack()
    with stack:
        def sb(name, shape, dt=F32):
            return stack.enter_context(nc.sbuf_tensor(name, shape, dt))

        def sem(name):
            return stack.enter_context(nc.semaphore(name))

        resid = sb("resid", [P, NT, P])
        shifted = sb("shifted", [P, NT + B, P])
        addend = sb("addend", [P, NT, P])
        xn = sb("xn", [P, NT + B, P])
        stats = sb("stats", [P, NT + B, 6])
        mv = sb("mv", [P, NT + B, 2])
        std = sb("std", [P, NT + B, 1])
        rstd = sb("rstd", [P, NT + B, 1])
        xT_hi = sb("xT_hi", [P, NT * P], F32R)
        xT_lo = sb("xT_lo", [P, NT * P], F32R)
        conv_w_sb = sb("conv_w_sb", [P, RATE, P])
        conv_x = sb("conv_x", [P, B, RATE, P])
        par = sb("par", [P, NSPLIT])
        par_hi = sb("par_hi", [P, NSPLIT], F32R)
        par_lo = sb("par_lo", [P, NSPLIT], F32R)
        const = sb("const", [P, NCONST])
        ident_bf = sb("ident_bf", [P, P], BF16)
        rows = sb("rows", [P, NROWS])
        bqk = sb("bqk", [STACK, 2 * GROUPS])
        eps = sb("eps", [P, 1])
        lg0 = sb("lg0", [P, NT, E0])
        pair_gt = sb("pair_gt", [P, NT, E0, E0], BF16)
        pair_eq = sb("pair_eq", [P, NT, E0, E0], BF16)
        tri_bf = sb("tri_bf", [P, E0 * E0], BF16)
        rank0 = sb("rank0", [P, NT, E0])
        first0 = sb("first0", [P, NT, E0])
        second0 = sb("second0", [P, NT, E0])
        chosen0 = sb("chosen0", [P, NT, E0])
        comb0 = sb("comb0", [P, NT, E0])
        tmp0 = sb("tmp0", [P, NT, E0])
        top0 = sb("top0", [P, 6, NT])
        parts0 = sb("parts0", [P, NT, 3, E0], BF16)
        combT0 = sb("combT0", [3 * E0, NT * P], BF16)
        gate1 = sb("gate1", [P, 4, NT, E1])
        key1, prob1, rest1 = (gate1[:, i, :, :] for i in range(3))
        mask1 = gate1[:, 3, :, :].rearrange("p n e -> p (n e)").bitcast(BF16)[:, 0:NT * E1]\
            .rearrange("p (n e) -> p n e", e=E1)
        ones_row = sb("ones_row", [1, P], F32R)
        eb_hi = sb("eb_hi", [1, E1], F32R)
        eb_lo = sb("eb_lo", [1, E1], F32R)
        best1 = sb("best1", [P, NT, TOP])
        scale1 = sb("scale1", [P, NT])
        parts1 = sb("parts1", [P, NT, KT * ROW_GROUPS, CELL], BF16)
        combT1 = sb("combT1", [P, KT, NT * P], BF16)
        k3 = sb("k3", [STACK, GROUPS, B, C])
        k3_part = sb("k3_part", [STACK, GROUPS, B, C], F32R)
        k_stack = sb("k_stack", [P, B, H, C], F32R)
        v_ones = sb("v_ones", [C, B, H, CELL])
        q_stack = sb("q_stack", [P, GROUPS, NT * P], F32R)
        nmax = sb("nmax", [P, NT, H])
        nmax_pad = sb("nmax_pad", [P, 2, P])
        NE = 8
        exps = gate1[0:C, :, :, :].rearrange("p a n e -> p (a n e)")[:, 0:NE * HALF]\
            .rearrange("p (i q) -> p i q", i=NE)
        turned = sb("turned", [P, 4 * HALF])
        pv_sb = turned[:, 0:2 * HALF].rearrange("p (i q) -> p i q", i=2)
        inv = sb("inv", [P, 2, NT // B, HG])
        onat = turned[:, 2 * HALF:4 * HALF].rearrange("p (n d) -> p n d", d=P)
        prob_parts1 = turned[:, :].bitcast(BF16)[:, 0:3 * NT * E1]\
            .rearrange("p (n c j e) -> p n c j e", n=NT, j=3, e=EC)
        oT = sb("oT", [P, NT * P])
        raw = [sb(f"raw{s}", [P, 1024]) for s in range(2)]
        w_hi = [sb(f"w_hi{s}", [P, 1024], F32R) for s in range(2)]
        w_lo = [sb(f"w_lo{s}", [P, 1024], F32R) for s in range(2)]
        sel = [sb(f"sel{s}", [P, P], BF16) for s in range(2)]
        silu_out = sb("silu_out", [P, 2, HALF])
        gated = sb("gated", [P, 2, HALF])
        hw = sb("hw", [P, 2, HALF])
        NH, RING = 4, 4
        h_hi = [sb(f"h_hi{i}", [P, HALF], F32R) for i in range(NH)]
        h_lo = [sb(f"h_lo{i}", [P, HALF], F32R) for i in range(NH)]
        waiting0 = [gated[:, 0, :], gated[:, 1, :], oT[:, 0:HALF], oT[:, HALF:2 * HALF]]
        waiting1 = [silu_out[:, 0, :], silu_out[:, 1, :], gated[:, 0, :], gated[:, 1, :]]
        shared_h = oT
        q_full = (gated[:, 0, :], gated[:, 1, :], hw[:, 0, :], hw[:, 1, :])
        yT = shifted[:, 0:NT, :].rearrange("p n d -> p (n d)")
        xT = yT

        psum = stack.enter_context(nc.psum_tensor("psum", [P, 8, HALF], F32))
        bank = [psum[:, i, :] for i in range(8)]
        acc = bank[6:8]

        def hi(name, a=0, b=None):
            s, e = SPLIT[name]
            return par_hi[:, s + a:(e if b is None else s + b)]

        def lo(name, a=0, b=None):
            s, e = SPLIT[name]
            return par_lo[:, s + a:(e if b is None else s + b)]

        def full(name):
            return par[:, slice(*SPLIT[name])]

        ident = const[:, IDENT:IDENT + P]

        rows_zeroed = sem("rows_zeroed")
        zeroed = sem("zeroed")
        parts1_zeroed = sem("parts1_zeroed")
        x_loaded = sem("x_loaded")
        shift_loaded = sem("shift_loaded")
        add_loaded = sem("add_loaded")
        conv_loaded = sem("conv_loaded")
        par_loaded = sem("par_loaded")
        const_loaded = sem("const_loaded")
        rows_loaded = sem("rows_loaded")
        eps_set = sem("eps_set")
        par_hi_ready = sem("par_hi_ready")
        par_lo_ready = sem("par_lo_ready")
        ident_cast = sem("ident_cast")
        dve_step = sem("dve_step")
        pool_step = sem("pool_step")
        var_ready = sem("var_ready")
        std_ready = sem("std_ready")
        xn_ready = sem("xn_ready")
        xT_psum = sem("xT_psum")
        xT_hi_ready = sem("xT_hi_ready")
        xT_lo_ready = sem("xT_lo_ready")
        convT_psum = sem("convT_psum")
        conv_x_ready = sem("conv_x_ready")
        conv_done = sem("conv_done")
        logits0 = sem("logits0")
        diff_ready = sem("diff_ready")
        exp_ready = sem("exp_ready")
        chosen_ready = sem("chosen_ready")
        place_ready = sem("place_ready")
        parts0_ready = sem("parts0_ready")
        combT0_psum = sem("combT0_psum")
        combT0_ready = sem("combT0_ready")
        k_psum = sem("k_psum")
        v_psum = sem("v_psum")
        k3_ready = sem("k3_ready")
        k_stack_ready = sem("k_stack_ready")
        v_ready = sem("v_ready")
        q_psum = sem("q_psum")
        q_hi_ready = sem("q_hi_ready")
        q_lo_ready = sem("q_lo_ready")
        q1_psum = sem("q1_psum")
        q1_hi_ready = sem("q1_hi_ready")
        q1_full_ready = sem("q1_full_ready")
        q1_lo_ready = sem("q1_lo_ready")
        scores_ready = sem("scores_ready")
        max_taken = sem("max_taken")
        nmax_ready = sem("nmax_ready")
        nmaxT_psum = sem("nmaxT_psum")
        q_max_ready = [sem(f"q_max_ready{b}") for b in range(B)]
        scoresT_ready = sem("scoresT_ready")
        exp_done = sem("exp_done")
        pv_done = sem("pv_done")
        pv_copied = sem("pv_copied")
        pv_turned = sem("pv_turned")
        onat_ready = sem("onat_ready")
        oT_psum = sem("oT_psum")
        oT_ready = [sem(f"oT_ready{b}") for b in range(B)]
        proj_done = sem("proj_done")
        logits1 = sem("logits1")
        xT_ready = [sem(f"xT_ready{half}") for half in range(2)]
        eb_hi_ready = sem("eb_hi_ready")
        eb_lo_ready = sem("eb_lo_ready")
        keys_ready = sem("keys_ready")
        prob_hi_ready = sem("prob_hi_ready")
        rest_ready = sem("rest_ready")
        prob_mid_ready = sem("prob_mid_ready")
        prob_low_ready = sem("prob_low_ready")
        parts1_ready = sem("parts1_ready")
        combT1_psum = sem("combT1_psum")
        combT1_dve = sem("combT1_dve")
        combT1_act = sem("combT1_act")
        prob_step = sem("prob_step")
        shared_gate = sem("shared_gate")
        shared_silu = sem("shared_silu")
        shared_down = sem("shared_down")
        sum1_ready = sem("sum1_ready")
        shared_added = sem("shared_added")
        yT_ready = [sem(f"yT_ready{i}") for i in range(2)]
        y_psum = sem("y_psum")
        out_ready = sem("out_ready")
        stored = sem("stored")

        class Stream:

            def __init__(self, tag, rounds, per, body, batch, two_gates, ahead, lag):
                self.tag, self.rounds, self.per, self.body, self.batch = tag, rounds, per, body, batch
                self.two_gates, self.ahead, self.lag = two_gates, ahead, lag
                self.units = rounds * per
                self.loaded = [sem(f"l{tag}_loaded{s}") for s in range(2)]
                self.sel_loaded = [sem(f"l{tag}_sel_loaded{s}") for s in range(2)]
                self.up_split = sem(f"l{tag}_up_split")
                self.down_split = sem(f"l{tag}_down_split")
                self.b_ready = sem(f"l{tag}_b_ready")
                self.a_ready = sem(f"l{tag}_a_ready")
                self.c_ready = sem(f"l{tag}_c_ready")
                self.silu = sem(f"l{tag}_silu")
                self.gated = sem(f"l{tag}_gated")
                self.hw = sem(f"l{tag}_hw")
                self.hi = sem(f"l{tag}_hi")
                self.lo = sem(f"l{tag}_lo")
                self.down = sem(f"l{tag}_down")

            def run(self, eng, body, rounds_per_body=None):
                body(0)
                with eng.Fori(1, self.rounds // (rounds_per_body or self.body)) as j:
                    body(j)

        s0 = Stream(0, E0, 2 * (HID0 // P), 2, HID0 // P, True, 2, 3)
        s1 = Stream(1, ROUNDS1, 2 * ROW_GROUPS, KT, 2, False, 2, 5)

        s0.up_read, s1.up_read = s0.a_ready, s1.b_ready
        s0.complete = (s0.down, s0.units)
        s1.complete = (s1.down, s1.units)

        def unit(s, v):
            if s is s0:
                half, part = divmod(v, HID0 // P)
                return (slice(HID0 + part * P, HID0 + part * P + P), slice(part * P, part * P + P),
                        slice(2 * HID0 + part * P, 2 * HID0 + part * P + P), half)
            half, part = v // 2 % 2, v // 4 * 2 + v % 2
            at = ROW_GROUPS * P + part * P
            return slice(part * P, part * P + P), None, slice(at, at + P), half

        def wait(eng, s, value):
            if not (isinstance(value, int) and value <= 0):
                eng.wait_ge(s, value)

        def known(j):
            return isinstance(j, int)

        NAT, TURN0 = 3, 2 * H - 8

        def head_bank(i):
            return (2, 3, 5)[i % 3] if i < H else (6, 7, 2, 3)[(i - H) % 4]

        def values_bank(n):
            return 4 if n < GROUPS else 5 - n % 2

        def last_in_bank(i):
            return max((j for j in range(i) if head_bank(j) == head_bank(i)), default=-1)

        def scores_part(n):
            if n < NT:
                return n // 2, n % 2 * 2, 2, 2 + n % 2 * 2
            t, g = divmod(n - NT, GROUPS)
            return NT // B + t, g, 1, 6 + n % 2

        def by_cell(a, t0, t1):
            return a[:, t0:t1, :].rearrange("p n (c e) -> p n c e", e=EC)

        block = stack.enter_context(nc.Block())

        @block.sync
        def _(sp):
            by_b = shifted[:, 0:NT, :].rearrange("p (b n) d -> p b n d", b=B)
            last = UNITS - NCONV - P
            first = T - UNITS - C - P
            x_by_row = x.rearrange("b t d -> t b d")
            for i, (dst, start, n) in enumerate(((by_b[:, :, 0, :], NCONV, P),
                                                 (by_b[:, :, 2, :], UNITS + C, P),
                                                 (shifted[0:CONV_ROWS, NT:NT + B, :], UNITS, CONV_ROWS),
                                                 (by_b[0:last, :, 1, :], NCONV + P, last),
                                                 (by_b[0:first, :, 3, :], UNITS + C + P, first))):
                if i == 2:
                    sp.wait_ge(rows_zeroed, 2)
                sp.dma_start(dst, x_by_row[start:start + n, :, :]).then_inc(shift_loaded, 16)
            sp.dma_start(resid[:, :, :], x.rearrange("b t d -> (b t) d").rearrange("(n p) d -> p n d", p=P))\
                .then_inc(x_loaded, 16)
            sp.dma_start(const[:, :], consts_in).then_inc(const_loaded, 16)
            sp.dma_start(conv_w_sb[:, :, :], conv_w.rearrange("r f o -> f r o")).then_inc(conv_loaded, 16)
            sp.wait_ge(zeroed, 1)
            by_b = addend[:, :, :].rearrange("p (b n) d -> p b n d", b=B)
            sp.dma_start(by_b[UNITS - NCONV - P:P, :, 1, :],
                         conv_b.unsqueeze(0).unsqueeze(0).broadcast_to([NCONV, B, P])).then_inc(add_loaded, 16)
            sp.dma_start(by_b[T - C - 3 * P:P, :, 3, :], ctx.rearrange("b c d -> c b d")).then_inc(add_loaded, 16)
            sp.dma_start(par[:, :], split_in).then_inc(par_loaded, 16)
            sp.dma_start(bqk[:, :], bqk_in).then_inc(rows_loaded, 16)
            sp.dma_start(rows[:, :], rows_in.broadcast_to([P, NROWS])).then_inc(rows_loaded, 16)

            def load(s, src, sel_src, cols, n_sel):
                def body(j):
                    for slot in range(2):
                        r = j * 2 + slot
                        batches = s.per // s.batch
                        wait(sp, s.down_split, j * 4 + 2 * (slot - 1))
                        if s is s1 and known(j):
                            sp.wait_ge(s0.c_ready, s0.units // s0.batch)
                            sp.wait_ge(s0.down_split, 2 * s0.rounds)
                        sp.dma_start(raw[slot][:, 0:cols], src[r, :, :]).then_inc(s.loaded[slot], 16)
                        wait(sp, s.c_ready, j * (2 * batches) + batches * (slot - 1))
                        sp.dma_start(sel[slot][0:n_sel, :], sel_src[r, :, :]).then_inc(s.sel_loaded[slot], 16)
                s.run(sp, body, 2)

            load(s0, w0_in, sel0_in.bitcast(BF16), 3 * HID0, 3 * E0)
            load(s1, w1_in, sel1_in.bitcast(BF16), 2 * ROW_GROUPS * P, P)
            for half in range(2):
                sp.wait_ge(out_ready, half + 1)
                n = NT // 2
                sp.dma_start(out.rearrange("b t d -> (b t) d").rearrange("(n p) d -> p n d", p=P)[:, half * n:half * n + n, :],
                             resid[:, half * n:half * n + n, :]).then_inc(stored, 16)
            sp.wait_ge(stored, 32)

        @block.gpsimd
        def _(pool):
            steps = [0]

            def step(ins):
                steps[0] += 1
                ins.then_inc(pool_step, 1)
                pool.wait_ge(pool_step, steps[0])

            pool.memset(shifted[:, 0:NT, :].rearrange("p (n two) d -> p n two d", two=2)[:, :, 1, :], 0.0)\
                .then_inc(rows_zeroed, 1)
            pool.memset(shifted[:, NT:NT + B, :], 0.0).then_inc(rows_zeroed, 1)
            pool.memset(addend[:, :, :], 0.0).then_inc(zeroed, 1)
            pool.memset(conv_x[:, :, :, :], 0.0).then_inc(zeroed, 1)
            pool.memset(nmax_pad[:, :, :], 0.0).then_inc(zeroed, 1)
            pool.memset(v_ones[:, :, :, :], 0.0).then_inc(zeroed, 1)
            pool.wait_ge(zeroed, 4)
            pool.memset(v_ones[:, :, :, D:D + 1], 1.0).then_inc(zeroed, 1)
            pool.wait_ge(par_loaded, 16)
            pool.wait_ge(par_hi_ready, 1)
            pool.tensor_tensor(par_lo[:, :], par[:, :], par_hi[:, :].bitcast(F32), ALU.subtract).then_inc(par_lo_ready, 1)
            pool.wait_ge(const_loaded, 16)
            pool.tensor_copy(ident_bf[:, :], ident).then_inc(ident_cast, 1)
            pool.tensor_copy(tri_bf[:, :], const[:, TRI:TRI + E0 * E0]).then_inc(ident_cast, 1)

            def split_part(slot, cols, done, count):
                pool.tensor_tensor(w_hi[slot][:, cols], raw[slot][:, cols],
                                   const[:, ONES:ONES + 1].broadcast_to([P, cols.stop - cols.start]), ALU.mult)\
                    .then_inc(done, 1)
                pool.wait_ge(done, count + 1)
                pool.tensor_tensor(w_lo[slot][:, cols], raw[slot][:, cols], w_hi[slot][:, cols].bitcast(F32),
                                   ALU.subtract).then_inc(done, 1)
                pool.wait_ge(done, count + 2)

            def split(s, up, down, between=None):
                def body(j):
                    for i in range(s.body):
                        slot = i % 2
                        r = j * s.body + i
                        if s is s1 and known(j) and i == 2:
                            between()
                        pool.wait_ge(s.loaded[slot], j * (8 * s.body) + (i // 2) * 16 + 16)
                        wait(pool, s.up_read, (r - 1) * s.per)
                        if s is s1 and known(j) and i < 2:
                            pool.wait_ge(s0.down, s0.units)
                        split_part(slot, slice(0, up), s.up_split, r * 2)
                        wait(pool, s.down, (r - 1) * s.per)
                        split_part(slot, slice(up, down), s.down_split, r * 2)
                s.run(pool, body)

            def stack_keys():
                pool.wait_ge(eb_hi_ready, 2)
                pool.tensor_tensor(eb_lo[:, :], rows[0:1, EB:EB + E1], eb_hi[:, :].bitcast(F32), ALU.subtract)\
                    .then_inc(eb_lo_ready, 1)
                pool.wait_ge(k3_ready, GROUPS)
                step(pool.tensor_tensor(k3_part[:, :, :, :].rearrange("p g b c -> p (g b c)"),
                                        k3[:, :, :, :].rearrange("p g b c -> p (g b c)"),
                                        const[0:STACK, ONES:ONES + 1].broadcast_to([STACK, GROUPS * B * C]), ALU.mult))
                low = slice(2 * HG * D, STACK)
                step(pool.tensor_tensor(k3_part[low, :, :, :], k3[low, :, :, :], k3_part[low, :, :, :].bitcast(F32),
                                        ALU.subtract))
                for b in range(B):
                    for g in range(GROUPS):
                        step(pool.tensor_tensor(
                            k_stack[0:STACK, b, g * HG:(g + 1) * HG, :],
                            k3_part[:, g, b, :].bitcast(F32).unsqueeze(1).broadcast_to([STACK, HG, C]),
                            const[0:STACK, HMASK:HMASK + HG].unsqueeze(2).broadcast_to([STACK, HG, C]), ALU.mult))
                    pool.tensor_tensor(k_stack[STACK:P, b, :, :],
                                       const[STACK:P, HSEL:HSEL + H].unsqueeze(2).broadcast_to([P - STACK, H, C]),
                                       const[STACK:P, ONES:ONES + 1].unsqueeze(2).broadcast_to([P - STACK, H, C]), ALU.mult)\
                        .then_inc(k_stack_ready, 1)
                    pool.wait_ge(k_stack_ready, b + 1)

            def between():
                mid = slice(HG * D, 2 * HG * D)
                for g in range(GROUPS):
                    pool.wait_ge(q1_hi_ready, g + 1)
                    pool.wait_ge(q1_full_ready, g + 1)
                    dst = q_stack[mid, g, T:2 * T]
                    pool.tensor_tensor(dst, q_full[g][mid, :], dst.bitcast(F32), ALU.subtract).then_inc(q1_lo_ready, 1)
                pool.wait_ge(q1_lo_ready, GROUPS)
                pool.memset(parts1[:, :, :, :], 0.0).then_inc(parts1_zeroed, 1)
                gate_rests()

            def gate_rests():
                def rest(k):
                    t0, t1 = GATE_SETS[k]
                    pool.wait_ge(prob_hi_ready, k + 1)
                    pool.tensor_tensor(by_cell(rest1, t0, t1), by_cell(prob1, t0, t1), prob_parts1[:, t0:t1, :, 0, :],
                                       ALU.subtract).then_inc(rest_ready, 1)

                def low(k):
                    t0, t1 = GATE_SETS[k]
                    pool.wait_ge(rest_ready, k + 1)
                    pool.wait_ge(prob_mid_ready, k + 1)
                    pool.tensor_tensor(prob_parts1[:, t0:t1, :, 2, :], by_cell(rest1, t0, t1),
                                       prob_parts1[:, t0:t1, :, 1, :], ALU.subtract).then_inc(prob_low_ready, 1)

                for half in range(2):
                    cols = slice(half * HALF, (half + 1) * HALF)
                    pool.wait_ge(xT_hi_ready, 4 + half + 1)
                    pool.tensor_tensor(xT_lo[:, cols], xT[:, cols], xT_hi[:, cols].bitcast(F32), ALU.subtract)\
                        .then_inc(xT_lo_ready, 1)
                last = len(GATE_SETS) - 1
                rest(0)
                for k in range(1, last + 1):
                    rest(k)
                    low(k - 1)
                low(last)

            split(s0, 2 * HID0, 3 * HID0)
            stack_keys()
            split(s1, ROW_GROUPS * P, 2 * ROW_GROUPS * P, between)

        @block.scalar
        def _(act):
            def ln_std(n, t0, t1):
                act.wait_ge(var_ready, n)
                act.activation(std[:, t0:t1, :], mv[:, t0:t1, 1:2], ACT.Sqrt, bias=eps[:, :]).then_inc(std_ready, 1)

            def ln_std_half(n, half):
                ln_std(2 * n + half - 1, half * NT // 2, (half + 1) * NT // 2)

            def high_half(n, half):
                act.wait_ge(xT_psum, 2 * (n - 1) + half + 1)
                act.activation(xT_hi[:, half * HALF:(half + 1) * HALF], bank[half], ACT.Copy).then_inc(xT_hi_ready, 1)

            def full_then_high(n, count):
                act.wait_ge(xT_psum, 2 * n - 1)
                act.activation(xT[:, 0:HALF], bank[0], ACT.Copy).then_inc(xT_ready[0], 1)
                for half in range(2):
                    act.wait_ge(xT_ready[half], count)
                    act.activation(xT_hi[:, half * HALF:(half + 1) * HALF], xT[:, half * HALF:(half + 1) * HALF],
                                   ACT.Copy).then_inc(xT_hi_ready, 1)

            def silu(s, u, v):
                wait(act, s.b_ready, u + v + 1)
                if s.two_gates:
                    dst = silu_out[:, v % 2, :]
                    wait(act, s.gated, u + v - 1)
                else:
                    dst = waiting1[v % RING]
                    wait(act, s.hw, u + v + 1 - RING)
                act.activation(dst, bank[(2 if s.two_gates else 0) + v % 2], ACT.Silu).then_inc(s.silu, 1)

            act.preload_act_table(ACT.Sqrt)
            act.wait_ge(eps_set, 1)
            ln_std(1, 0, NT + B)
            act.wait_ge(par_loaded, 16)
            act.activation(par_hi[:, :], par[:, :], ACT.Copy).then_inc(par_hi_ready, 1)
            ln_std(2, 0, NT)
            full_then_high(1, 1)
            act.wait_ge(rows_loaded, 32)
            for g in range(GROUPS):
                act.wait_ge(k_psum, g // 2 * 2 + 2)
                act.activation(k3[:, g, :, :], bank[2 + g // 2][0:STACK, (g % 2) * B * C:(g % 2 + 1) * B * C]
                               .rearrange("p (b c) -> p b c", b=B),
                               ACT.Identity, bias=bqk[:, GROUPS + g:GROUPS + g + 1]).then_inc(k3_ready, 1)
            act.preload_act_table(ACT.Silu)
            silu(s0, 0, 0)
            act.preload_act_table(ACT.Exp)
            act.wait_ge(diff_ready, 1)
            act.activation(top0[:, 3, :], top0[:, 2, :], ACT.Exp).then_inc(exp_ready, 1)
            act.wait_ge(const_loaded, 16)
            act.activation(ones_row[:, :], const[0:1, ONES:ONES + P], ACT.Copy).then_inc(eb_hi_ready, 1)
            act.activation(eb_hi[:, :], rows[0:1, EB:EB + E1], ACT.Copy).then_inc(eb_hi_ready, 1)

            def stream(s, before_high=None):
                def high(u, v):
                    wait(act, s.hw, u + v + 1)
                    wait(act, s.down, u + v + 1 - NH)
                    act.activation(h_hi[v % NH][:, :], hw[:, v % 2, :], ACT.Copy).then_inc(s.hi, 1)

                def body(j):
                    u = j * (s.body * s.per)
                    for v in range(s.body * s.per):
                        if not (s is s0 and known(j) and v == 0):
                            silu(s, u, v)
                        if known(j) and v == s.ahead and before_high:
                            before_high()
                            high(u, 0)
                        elif not known(j) or v > s.ahead + (1 if before_high else 0):
                            high(u, v - s.ahead - 1)
                s.run(act, body)
                for v in range(-s.ahead - 1, 0):
                    high(s.units, v)
                act.wait_ge(*s.complete)
                act.activation(yT[:, 0:HALF], acc[0], ACT.Copy).then_inc(yT_ready[0], 1)

            stream(s0)
            act.preload_act_table(ACT.Sqrt)
            ln_std_half(2, 0)
            high_half(2, 0)
            ln_std_half(2, 1)
            for g in range(GROUPS):
                act.wait_ge(q_psum, g + 1)
                act.activation(q_stack[0:STACK, g, 0:T], bank[2 + g][0:STACK, :], ACT.Identity,
                               bias=bqk[:, g:g + 1]).then_inc(q_hi_ready, 1)
            high_half(2, 1)
            act.preload_act_table(ACT.Exp)
            mid = slice(HG * D, 2 * HG * D)
            for g in range(GROUPS):
                act.wait_ge(q1_psum, g + 1)
                act.activation(q_stack[0:STACK, g, T:2 * T], bank[6 + g % 2][0:STACK, :], ACT.Identity,
                               bias=bqk[:, g:g + 1]).then_inc(q1_hi_ready, 1)
                act.activation(q_full[g][mid, :], bank[6 + g % 2][mid, :], ACT.Identity,
                               bias=bqk[mid, g:g + 1]).then_inc(q1_full_ready, 1)

            def maxima(g):
                act.wait_ge(nmaxT_psum, NT // B)
                act.activation(q_stack[STACK:P, g, 0:T], bank[0][STACK:P, :], ACT.Copy).then_inc(q_max_ready[0], 1)

            maxima(0)
            maxima(1)
            for i in range(B * H):
                if i in (2, 4):
                    maxima(1 + i // 2)
                act.wait_ge(scoresT_ready, i + 1)
                wait(act, pv_done, i // HG - 1)
                act.activation(exps[:, i % NE, :], bank[head_bank(i)][0:C, :], ACT.Exp, scale=SCALE).then_inc(exp_done, 1)
                if i % HG == 2 and HG < i < H + HG:
                    n = i // HG - 1
                    act.wait_ge(pv_done, n + 1)
                    wait(act, pv_turned, n - 1)
                    act.activation(pv_sb[:, n % 2, :], bank[values_bank(n)], ACT.Copy).then_inc(pv_copied, 1)
            act.wait_ge(oT_psum, 2)
            act.activation(oT[:, T:2 * T], bank[1], ACT.Copy).then_inc(oT_ready[1], 1)
            act.preload_act_table(ACT.Sqrt)
            for half in range(2):
                ln_std_half(3, half)
            full_then_high(3, 2)
            act.preload_act_table(ACT.Sigmoid)

            def sigmoid(k):
                t0, t1 = GATE_SETS[k]
                act.wait_ge(keys_ready, k + 1)
                act.activation(prob1[:, t0:t1, :], bank[2 + k][:, 0:(t1 - t0) * E1].rearrange("p (n e) -> p n e", e=E1),
                               ACT.Sigmoid).then_inc(prob_step, 1)
                act.wait_ge(prob_step, k + 1)
                act.activation(prob_parts1[:, t0:t1, :, 0, :], by_cell(prob1, t0, t1), ACT.Copy).then_inc(prob_hi_ready, 1)

            def middle(k):
                t0, t1 = GATE_SETS[k]
                act.wait_ge(rest_ready, k + 1)
                act.activation(prob_parts1[:, t0:t1, :, 1, :], by_cell(rest1, t0, t1), ACT.Copy)\
                    .then_inc(prob_mid_ready, 1)

            last = len(GATE_SETS) - 1
            sigmoid(0)
            for k in range(1, last + 1):
                sigmoid(k)
                middle(k - 1)
            middle(last)
            for half in range(2):
                act.wait_ge(shared_gate, half + 1)
                act.activation(shared_h[:, half * HALF:(half + 1) * HALF], acc[half], ACT.Silu)\
                    .then_inc(shared_silu, 1)

            def copy_combT():
                for k in (2, 3):
                    act.wait_ge(combT1_psum, k + 1)
                    act.activation(combT1[:, k, :], bank[2 + k].bitcast(BF16), ACT.Copy).then_inc(combT1_act, 1)
            stream(s1, copy_combT)

        @block.vector
        def _(dve):
            steps = [0]

            def step(ins):
                steps[0] += 1
                ins.then_inc(dve_step, 1)
                dve.wait_ge(dve_step, steps[0])

            def statistics(src, tiles):
                for t in tiles:
                    last = dve.bn_stats(stats[:, t, :], src[:, t, :])
                step(last)
                for t in tiles:
                    last = dve.bn_aggr(mv[:, t, :], stats[:, t, :])
                return last

            def normalise(n, src, t0, t1, order, after_five=None):
                dve.wait_ge(std_ready, n)
                step(dve.reciprocal(rstd[:, t0:t1, :], std[:, t0:t1, :]))
                for i, t in enumerate(order):
                    if i == 5 and after_five:
                        after_five()
                    dve.tensor_scalar(xn[:, t, :], src[:, t, :], mv[:, t, 0:1], rstd[:, t, :], ALU.subtract, ALU.mult)\
                        .then_inc(xn_ready, 1)

            def statistics_half(half):
                statistics(resid, range(half * NT // 2, (half + 1) * NT // 2)).then_inc(var_ready, 1)

            def normalise_half(n, half):
                t0, t1 = half * NT // 2, (half + 1) * NT // 2
                normalise(2 * n + half - 1, resid, t0, t1, range(t0, t1))

            def low_half(n, half):
                cols = slice(half * HALF, (half + 1) * HALF)
                dve.wait_ge(xT_hi_ready, 2 * (n - 1) + half + 1)
                dve.tensor_tensor(xT_lo[:, cols], bank[half], xT_hi[:, cols].bitcast(F32), ALU.subtract)\
                    .then_inc(xT_lo_ready, 1)

            def conv_operand():
                dve.wait_ge(convT_psum, 1)
                dve.wait_ge(zeroed, 2)
                at = UNITS - NCONV - P
                dve.tensor_copy(conv_x[:, :, :, at:P],
                                bank[0][:, 0:B * P].rearrange("p (b m) -> p b m", b=B)[:, :, 0:CONV_ROWS]
                                .rearrange("p b (j r) -> p b r j", r=RATE)).then_inc(conv_x_ready, 1)

            dve.memset(eps[:, :], EPS).then_inc(eps_set, 1)
            dve.wait_ge(shift_loaded, 16 * 5)
            statistics(shifted, range(NT + B)).then_inc(var_ready, 1)
            normalise(1, shifted, 0, NT + B, list(range(NT, NT + B)) + list(range(NT)), after_five=conv_operand)
            dve.wait_ge(x_loaded, 16)
            dve.wait_ge(xn_ready, NT + B)
            step(dve.tensor_tensor(resid[:, :, :], resid[:, :, :], xn[:, 0:NT, :], ALU.add))
            dve.wait_ge(add_loaded, 16 * 2)
            odd = resid[:, :, :].rearrange("p (n two) d -> p n two d", two=2)[:, :, 1, :]
            step(dve.tensor_tensor(odd, odd, addend[:, :, :].rearrange("p (n two) d -> p n two d", two=2)[:, :, 1, :],
                                   ALU.add))
            with_conv = range(1, NT, NT // B)
            statistics(resid, [t for t in range(NT) if t not in with_conv])
            dve.wait_ge(conv_done, 1)
            conv_tiles = resid[:, :, :].rearrange("p (b n) d -> p b n d", b=B)[:, :, 1, :]
            step(dve.tensor_tensor(conv_tiles, conv_tiles, bank[1][:, 0:B * P].rearrange("p (b d) -> p b d", b=B),
                                   ALU.add))

            statistics(resid, with_conv).then_inc(var_ready, 1)
            normalise(2, resid, 0, NT, range(NT))
            dve.wait_ge(xT_psum, 2)
            dve.tensor_copy(xT[:, HALF:2 * HALF], bank[1]).then_inc(xT_ready[1], 1)
            for half in range(2):
                cols = slice(half * HALF, (half + 1) * HALF)
                dve.wait_ge(xT_hi_ready, half + 1)
                dve.wait_ge(xT_ready[half], 1)
                dve.tensor_tensor(xT_lo[:, cols], xT[:, cols], xT_hi[:, cols].bitcast(F32), ALU.subtract)\
                    .then_inc(xT_lo_ready, 1)
            dve.wait_ge(v_psum, 1)
            dve.wait_ge(zeroed, 5)
            dve.wait_ge(rows_loaded, 32)
            for b in range(B):
                dve.tensor_tensor(v_ones[:, b, :, 0:D],
                                  bank[4][0:C, b * P:(b + 1) * P].rearrange("p (h d) -> p h d", h=H),
                                  rows[0:C, BV:BV + P].rearrange("p (h d) -> p h d", h=H), ALU.add).then_inc(v_ready, 1)
            dve.wait_ge(logits0, 1)
            step(dve.tensor_tensor(lg0[:, :, :], bank[5][:, 0:NT * E0].rearrange("p (n e) -> p n e", n=NT),
                                   rows[:, RB0:RB0 + E0].unsqueeze(1).broadcast_to([P, NT, E0]), ALU.add))

            def gate(u, v):
                wait(dve, s0.silu, u + v + 1)
                wait(dve, s0.a_ready, u + v + 1)
                dve.tensor_tensor(waiting0[v % RING], silu_out[:, v % 2, :], bank[v % 2], ALU.mult)\
                    .then_inc(s0.gated, 1)

            other = lg0[:, :, :].unsqueeze(2).broadcast_to([P, NT, E0, E0])
            own = lg0[:, :, :].unsqueeze(3).broadcast_to([P, NT, E0, E0])
            dve.tensor_tensor(pair_gt[:, :, :, :], other, own, ALU.is_gt)
            step(dve.tensor_tensor(pair_eq[:, :, :, :], other, own, ALU.is_equal))
            flat = "p n a b -> p n (a b)"
            dve.wait_ge(ident_cast, 2)
            step(dve.tensor_tensor(pair_eq[:, :, :, :].rearrange(flat), pair_eq[:, :, :, :].rearrange(flat),
                                   tri_bf[:, :].unsqueeze(1).broadcast_to([P, NT, E0 * E0]), ALU.mult))
            step(dve.tensor_tensor(pair_gt[:, :, :, :], pair_gt[:, :, :, :], pair_eq[:, :, :, :], ALU.add))
            step(dve.tensor_reduce(rank0[:, :, :], pair_gt[:, :, :, :], AX.X, ALU.add))
            dve.tensor_scalar(chosen0[:, :, :], rank0[:, :, :], 2.0, None, ALU.is_lt).then_inc(chosen_ready, 1)
            dve.tensor_scalar(second0[:, :, :], rank0[:, :, :], 1.0, None, ALU.is_equal)
            dve.tensor_scalar(first0[:, :, :], rank0[:, :, :], 0.0, None, ALU.is_equal)
            step(dve.tensor_reduce(top0[:, 0, :], lg0[:, :, :], AX.X, ALU.max))
            step(dve.tensor_tensor(tmp0[:, :, :], lg0[:, :, :], second0[:, :, :], ALU.mult))
            step(dve.tensor_reduce(top0[:, 1, :], tmp0[:, :, :], AX.X, ALU.add))
            dve.tensor_tensor(top0[:, 2, :], top0[:, 1, :], top0[:, 0, :], ALU.subtract).then_inc(diff_ready, 1)
            dve.wait_ge(exp_ready, 1)
            step(dve.tensor_scalar(top0[:, 4, :], top0[:, 3, :], 1.0, None, ALU.add))
            step(dve.reciprocal(top0[:, 4, :], top0[:, 4, :]))
            step(dve.tensor_tensor(top0[:, 5, :], top0[:, 3, :], top0[:, 4, :], ALU.mult))
            dve.tensor_tensor(first0[:, :, :], first0[:, :, :],
                              top0[:, 4, :].unsqueeze(2).broadcast_to([P, NT, E0]), ALU.mult)
            step(dve.tensor_tensor(second0[:, :, :], second0[:, :, :],
                                   top0[:, 5, :].unsqueeze(2).broadcast_to([P, NT, E0]), ALU.mult))
            step(dve.tensor_tensor(comb0[:, :, :], first0[:, :, :], second0[:, :, :], ALU.add))
            gate(0, 0)
            dve.wait_ge(place_ready, 1)
            step(dve.scalar_tensor_tensor(comb0[:, :, :], bank[4][:, 256:256 + NT * E0].rearrange("p (n e) -> p n e", n=NT),
                                          float(CAPACITY), comb0[:, :, :], ALU.is_lt, ALU.mult))
            rest = tmp0[:, :, :]
            step(dve.tensor_copy(parts0[:, :, 0, :], comb0[:, :, :]))
            step(dve.tensor_tensor(rest, comb0[:, :, :], parts0[:, :, 0, :], ALU.subtract))
            step(dve.tensor_copy(parts0[:, :, 1, :], rest))
            dve.tensor_tensor(parts0[:, :, 2, :], rest, parts0[:, :, 1, :], ALU.subtract).then_inc(parts0_ready, 1)
            for v in range(1, s0.ahead):
                gate(0, v)
            dve.wait_ge(combT0_psum, 1)
            dve.tensor_copy(combT0[:, :], bank[6].bitcast(BF16)[0:3 * E0, :]).then_inc(combT0_ready, 1)

            def stream(s, beside=None):
                def weigh(u, c, v):
                    wait(dve, s.gated if s.two_gates else s.silu, u + v + 1)
                    wait(dve, s.c_ready, c + v // s.batch + 1)
                    wait(dve, s.hi, u + v - 1)
                    wait(dve, s.lo, u + v - 1)
                    dve.tensor_tensor(hw[:, v % 2, :], (waiting0 if s.two_gates else waiting1)[v % RING],
                                      bank[4 + v // s.batch % 2 if s.two_gates else 2 + v % ROW_GROUPS], ALU.mult)\
                        .then_inc(s.hw, 1)

                def low(u, v):
                    wait(dve, s.hi, u + v + 1)
                    dve.tensor_tensor(h_lo[v % NH][:, :], hw[:, v % 2, :], h_hi[v % NH][:, :].bitcast(F32),
                                      ALU.subtract).then_inc(s.lo, 1)

                def body(j):
                    u, c = j * (s.body * s.per), j * (s.body * s.per // s.batch)
                    for v in range(s.body * s.per):
                        w = v - s.ahead
                        if s.two_gates and not (known(j) and v < s.ahead):
                            gate(u, v)
                        if not known(j) or w >= 0:
                            weigh(u, c, w)
                        if known(j) and beside:
                            beside(w)
                        if not known(j) or w >= 1:
                            low(u, w - 1)
                s.run(dve, body)
                for w in range(-s.ahead, 0):
                    weigh(s.units, s.units // s.batch, w)
                    low(s.units, w - 1)
                low(s.units, -1)
                dve.wait_ge(*s.complete)
                dve.tensor_copy(yT[:, HALF:2 * HALF], acc[1]).then_inc(yT_ready[1], 1)

            stream(s0)

            def add_half(half, at, ready, value):
                part = resid[:, half * NT // 2:(half + 1) * NT // 2, :]
                dve.wait_ge(ready, value)
                step(dve.tensor_tensor(part, part, bank[at].rearrange("p (n d) -> p n d", d=P), ALU.add))

            add_half(0, 0, y_psum, 1)
            statistics_half(0)
            add_half(1, 1, y_psum, 2)
            normalise_half(2, 0)
            statistics_half(1)
            low_half(2, 0)
            normalise_half(2, 1)
            mid = slice(HG * D, 2 * HG * D)
            for g in range(GROUPS):
                dve.wait_ge(q_hi_ready, g + 1)
                dst = q_stack[mid, g, 0:T]
                dve.scalar_tensor_tensor(dst, bank[2 + g][mid, :], bqk[mid, g:g + 1], dst.bitcast(F32),
                                         ALU.add, ALU.subtract).then_inc(q_lo_ready, 1)
            low_half(2, 1)

            def take_max(n):
                t, g, count, at = scores_part(n)
                dve.wait_ge(scores_ready, n + 1)
                dve.tensor_reduce(nmax[:, t, g * HG:(g + count) * HG].rearrange("p (k h) -> p k h", k=count),
                                  psum[:, at:at + count, 0:HG * C].rearrange("p k (h c) -> p k h c", h=HG),
                                  AX.X, ALU.max, negate=True).then_inc(max_taken, 1)
                if g + count < GROUPS:
                    return
                dve.wait_ge(max_taken, n + 1)
                wait(dve, nmaxT_psum, t - 1)
                dst = nmax_pad[:, t % 2, STACK:STACK + H]
                step(dve.tensor_copy(dst.bitcast(F32R), nmax[:, t, :]))
                dve.tensor_tensor(nmax_pad[:, t % 2, STACK + H:P].bitcast(F32R), nmax[:, t, :], dst, ALU.subtract)\
                    .then_inc(nmax_ready, 1)

            def normalise_group(n):
                b, g = divmod(n, GROUPS)
                t0 = b * (NT // B)
                dve.wait_ge(pv_turned, n + 1)
                pv = bank[0].rearrange("p (t h d) -> p t h d", t=NT // B, h=HG)
                step(dve.reciprocal(inv[:, n % 2, :, :], pv[:, :, :, D]))
                dve.tensor_tensor(onat[:, t0:t0 + NT // B, g * HG * D:(g + 1) * HG * D].rearrange("p t (h d) -> p t h d", h=HG),
                                  pv[:, :, :, 0:D],
                                  inv[:, n % 2, :, :].unsqueeze(3).broadcast_to([P, NT // B, HG, D]), ALU.mult)\
                    .then_inc(onat_ready, 1)

            def copy_group(n):
                dve.wait_ge(pv_done, n + 1)
                wait(dve, pv_turned, n - 1)
                dve.tensor_copy(pv_sb[:, n % 2, :], bank[values_bank(n)]).then_inc(pv_copied, 1)

            for n in range(NT):
                take_max(n)
            for i in range(B * H):
                if NAT <= i < NAT + NT:
                    for k in range(2):
                        take_max(NT + 2 * (i - NAT) + k)
                if i % HG == HG - 1 and i >= H + HG:
                    copy_group(i // HG - 1)
                if i % HG == 0 and i >= 3 * HG:
                    normalise_group(i // HG - 3)
                if NAT + NT + 2 <= i < NAT + NT + 2 + GROUPS:
                    g = i - NAT - NT - 2
                    dve.wait_ge(nmaxT_psum, NT)
                    dve.tensor_copy(q_stack[STACK:P, g, T:2 * T], bank[1][STACK:P, :]).then_inc(q_max_ready[1], 1)
                if i == H + 1:
                    step(dve.tensor_tensor(resid[:, :, :], resid[:, :, :],
                                           rows[:, BO:BO + P].unsqueeze(1).broadcast_to([P, NT, P]), ALU.add))
                if i == TURN0 + 1:
                    dve.wait_ge(oT_psum, 1)
                    dve.tensor_copy(oT[:, 0:T], bank[1]).then_inc(oT_ready[0], 1)
                if i == TURN0 + 4:
                    add_half(0, 1, proj_done, 1)
            normalise_group(B * GROUPS - 3)
            copy_group(B * GROUPS - 1)
            normalise_group(B * GROUPS - 2)
            normalise_group(B * GROUPS - 1)
            statistics_half(0)
            add_half(1, 0, proj_done, 2)

            statistics_half(1)
            for half in range(2):
                normalise_half(3, half)
            dve.wait_ge(xT_psum, 6)
            dve.tensor_copy(xT[:, HALF:2 * HALF], bank[1]).then_inc(xT_ready[1], 1)

            def choose(k):
                t0, t1 = GATE_SETS[k]
                dve.wait_ge(logits1, k + 1)
                dve.tensor_scalar(key1[:, t0:t1, :], bank[2 + k][:, 0:(t1 - t0) * E1].rearrange("p (n e) -> p n e", e=E1),
                                  SIG_LOW, SIG_HIGH, ALU.max, ALU.min).then_inc(keys_ready, 1)
                dve.wait_ge(keys_ready, k + 1)
                for t in range(t0, t1):
                    last = dve.max(best1[:, t, :], key1[:, t, :])
                step(last)
                for t in range(t0, t1):
                    last = dve.match_replace(key1[:, t, :], best1[:, t, :], key1[:, t, :], -3e38)
                step(last)
                step(dve.tensor_scalar(mask1[:, t0:t1, :], key1[:, t0:t1, :], -1e38, None, ALU.is_lt))

            def keep_chosen(k):
                t0, t1 = GATE_SETS[k]
                dve.wait_ge(prob_low_ready, k + 1)
                shape = [P, (t1 - t0) * KT * ROW_GROUPS, 3, EC]
                dve.tensor_tensor(parts1[:, t0:t1, :, 0:3 * EC].rearrange("p n c (j e) -> p (n c) j e", e=EC),
                                  prob_parts1[:, t0:t1, :, :, :].rearrange("p n c j e -> p (n c) j e"),
                                  mask1[:, t0:t1, :].rearrange("p n (c e) -> p (n c) e", e=EC).unsqueeze(2)
                                  .broadcast_to(shape), ALU.mult).then_inc(parts1_ready, 1)

            dve.wait_ge(parts1_zeroed, 1)
            for k in range(len(GATE_SETS)):
                choose(k)
            for k in range(len(GATE_SETS)):
                keep_chosen(k)
            for k in (0, 1):
                dve.wait_ge(combT1_psum, k + 1)
                dve.tensor_copy(combT1[:, k, :], bank[2 + k].bitcast(BF16)).then_inc(combT1_dve, 1)

            def add_shared():
                dve.wait_ge(shared_down, 1)
                for half in range(2):
                    part = resid[:, half * NT // 2:(half + 1) * NT // 2, :]
                    last = dve.tensor_tensor(part, part, acc[half].rearrange("p (n d) -> p n d", d=P), ALU.add)
                last.then_inc(shared_added, 1)

            def beside(v):
                if v == 1:
                    add_shared()
                if 4 <= v < 4 + NT:
                    t = v - 4
                    dve.scalar_tensor_tensor(rest1[:, t, :], key1[:, t, :], -1e38, prob1[:, t, :],
                                             ALU.is_lt, ALU.mult, accum_out=scale1[:, t:t + 1]).then_inc(sum1_ready, 1)
                if v == 4 + NT:
                    dve.wait_ge(sum1_ready, NT)
                    step(dve.tensor_scalar(scale1[:, :], scale1[:, :], 1e-9, None, ALU.add))
                    step(dve.reciprocal(scale1[:, :], scale1[:, :]))
                    step(dve.tensor_scalar(scale1[:, :], scale1[:, :], ROUTED_SCALE, None, ALU.mult))

            stream(s1, beside)
            dve.wait_ge(shared_added, 1)
            for half in range(2):
                dve.wait_ge(y_psum, 2 + half + 1)
                for t in range(half * NT // 2, (half + 1) * NT // 2):
                    last = dve.scalar_tensor_tensor(resid[:, t, :], bank[half][:, (t % 4) * P:(t % 4 + 1) * P],
                                                    scale1[:, t:t + 1], resid[:, t, :], ALU.mult, ALU.add)
                last.then_inc(out_ready, 1)

        @block.tensor
        def _(pe):
            mm = nc.tensor.matmul

            def three(dst, w, rhs, start, stop):
                (wh, wl), (rh, rl) = w, rhs
                mm(dst, wh, rh, start=start, stop=False)
                mm(dst, wh, rl, start=False, stop=False)
                return mm(dst, wl, rh, start=False, stop=stop)

            def cols(half):
                c = slice(half * HALF, (half + 1) * HALF)
                return xT_hi[:, c], xT_lo[:, c]

            def transpose_rows(before, t0=0, t1=NT):
                for t in range(t0, t1):
                    pe.wait_ge(xn_ready, before + t + 1)
                    last = nc.tensor.transpose(bank[t // 4][:, (t % 4) * P:(t % 4 + 1) * P], xn[:, t, :], ident)
                    if t % 4 == 3:
                        last.then_inc(xT_psum, 1)

            pe.wait_ge(const_loaded, 16)
            for b in range(B):
                pe.wait_ge(xn_ready, b + 1)
                last = nc.tensor.transpose(bank[0][:, b * P:(b + 1) * P], xn[:, NT + b, :], ident)
            last.then_inc(convT_psum, 1)
            pe.wait_ge(conv_x_ready, 1)
            pe.wait_ge(conv_loaded, 16)
            for b in range(B):
                for r in range(RATE):
                    last = mm(bank[1][:, b * P:(b + 1) * P], conv_x[:, b, r, :], conv_w_sb[:, r, :],
                              start=r == 0, stop=r == RATE - 1)
            last.then_inc(conv_done, 1)
            pe.wait_ge(par_hi_ready, 1)
            pe.wait_ge(par_lo_ready, 1)
            for g in range(GROUPS):
                c = (g * STACK, (g + 1) * STACK)
                three(bank[2 + g // 2][0:STACK, (g % 2) * B * C:(g % 2 + 1) * B * C],
                      (hi("wk", *c), lo("wk", *c)), (hi("ctxT"), lo("ctxT")), True, True).then_inc(k_psum, 1)
            for b in range(B):
                c = (b * C, (b + 1) * C)
                last = three(bank[4][0:C, b * P:(b + 1) * P], (hi("ctxT", *c), lo("ctxT", *c)), (hi("wv"), lo("wv")),
                             True, True)
            last.then_inc(v_psum, 1)

            transpose_rows(NT + B)
            for t in range(NT):
                pe.wait_ge(xT_ready[t // 4], 1)
                last = mm(bank[5][:, t * E0:(t + 1) * E0], xT[:, t * P:(t + 1) * P], full("rw0"), start=True, stop=True)
            last.then_inc(logits0, 1)

            def places():
                pe.wait_ge(chosen_ready, 1)
                pe.wait_ge(v_ready, B)
                place = bank[4][:, 256:256 + NT * E0]
                picks = chosen0[:, :, :].rearrange("p n e -> p (n e)")
                mm(place, const[:, ULT:ULT + P], picks, start=True, stop=False)
                for d in range(1, NT):
                    last = mm(place[:, d * E0:], const[:, ONES:ONES + P], picks[:, 0:(NT - d) * E0], start=False,
                              stop=d == NT - 1)
                last.then_inc(place_ready, 1)

            def turn_comb0():
                pe.wait_ge(parts0_ready, 1)
                pe.wait_ge(ident_cast, 2)
                for t in range(NT):
                    last = nc.tensor.transpose(bank[6].bitcast(BF16)[0:3 * E0, t * P:(t + 1) * P],
                                               parts0[:, t, :, :].rearrange("p j e -> p (j e)"), ident_bf[:, :])
                last.then_inc(combT0_psum, 1)
                pe.wait_ge(combT0_ready, 1)

            def stream(s, before_combine, after_combine=None, early=None):
                def up(j, u, v):
                    i, r = v // s.per, v % 2
                    slot = i % 2
                    gate, lin, _, half = unit(s, v % s.per)
                    if v % s.per == 0:
                        pe.wait_ge(s.up_split, j * (2 * s.body) + 2 * i + 2)
                    wait(pe, s.silu, u + v - 1)
                    three(bank[(2 if s.two_gates else 0) + r], (w_hi[slot][:, gate], w_lo[slot][:, gate]), cols(half),
                          True, True).then_inc(s.b_ready, 1)
                    if s.two_gates:
                        wait(pe, s.gated, u + v - 1)
                        three(bank[r], (w_hi[slot][:, lin], w_lo[slot][:, lin]), cols(half), True, True)\
                            .then_inc(s.a_ready, 1)

                def combine(j, u, v):
                    i = v // s.per
                    slot = i % 2
                    _, _, _, half = unit(s, v % s.per)
                    c = slice(half * HALF, (half + 1) * HALF)
                    if v % s.per == 0:
                        pe.wait_ge(s.sel_loaded[slot], j * (8 * s.body) + (i // 2) * 16 + 16)
                    wait(pe, s.hw, u + v - s.batch)
                    if s.two_gates:
                        mm(bank[4 + v // s.batch % 2], sel[slot][0:3 * E0, :], combT0[:, c], start=True, stop=True)\
                            .then_inc(s.c_ready, 1)
                        return
                    if known(j) and v == 2:
                        pe.wait_ge(combT1_act, 2)
                    for w in range(v, v + s.batch):
                        g = w % s.per // 4 * 2 + w % 2
                        k = slice(g * CELL, g * CELL + 3 * EC)
                        last = mm(bank[2 + w % 4], sel[slot][k, :], combT1[k, i % s.body, c], start=True, stop=True)
                    last.then_inc(s.c_ready, 1)

                def down(j, u, v, first=False, last=False):
                    slot = (v // s.per) % 2
                    _, _, cols_down, half = unit(s, v % s.per)
                    if v % s.per == 0:
                        pe.wait_ge(s.down_split, j * (2 * s.body) + 2 * (v // s.per) + 2)
                    if s is s1 and first:
                        pe.wait_ge(shared_added, 1)
                    wait(pe, s.lo, u + v + 1)
                    three(acc[half], (w_hi[slot][:, cols_down], w_lo[slot][:, cols_down]),
                          (h_hi[v % NH][:, :], h_lo[v % NH][:, :]), first, last)\
                        .then_inc(s.down, 1)

                def body(j):
                    u = j * (s.body * s.per)
                    for v in range(s.body * s.per):
                        up(j, u, v)
                        w = v - s.ahead
                        x = w - s.lag
                        if known(j) and v == 1 and early:
                            early()
                        if known(j) and w < 0:
                            continue
                        if known(j) and w == 0:
                            before_combine()
                            combine(j, u, w)
                            if after_combine:
                                after_combine()
                        elif s.two_gates and w % s.batch == 0:
                            combine(j, u, w)
                        if not known(j) or x >= 0:
                            down(j, u, x, first=known(j) and x in (0, 2))
                        if not s.two_gates and w % s.batch == 0 and not (known(j) and w == 0):
                            combine(j, u, w)
                s.run(pe, body)
                for w in range(-s.ahead, s.lag):
                    if w < 0 and w % s.batch == 0:
                        combine(s.rounds // s.body, s.units, w)
                    down(s.rounds // s.body, s.units, w - s.lag, last=w - s.lag in (-3, -1))

            def transpose_back(n):
                for t in range(NT):
                    pe.wait_ge(yT_ready[t // 4], n + 1)
                    last = nc.tensor.transpose(bank[t // 4][:, (t % 4) * P:(t % 4 + 1) * P], yT[:, t * P:(t + 1) * P],
                                               ident)
                    if t % 4 == 3:
                        last.then_inc(y_psum, 1)

            pe.wait_ge(xT_lo_ready, 2)
            pe.wait_ge(k3_ready, GROUPS)
            stream(s0, turn_comb0, early=places)
            transpose_back(0)

            transpose_rows(2 * NT + B, 0, NT // 2)
            for g in range(GROUPS):
                c = (g * STACK, (g + 1) * STACK)
                pe.wait_ge(xT_lo_ready, 3)
                three(bank[2 + g][0:STACK, :], (hi("wq", *c), lo("wq", *c)), cols(0), True, True).then_inc(q_psum, 1)
            transpose_rows(2 * NT + B, NT // 2, NT)

            def queries1(g):
                c = (g * STACK, (g + 1) * STACK)
                pe.wait_ge(xT_lo_ready, 4)
                wait(pe, q1_full_ready, g - 1)
                three(bank[6 + g % 2][0:STACK, :], (hi("wq", *c), lo("wq", *c)), cols(1), True, True).then_inc(q1_psum, 1)

            def scores(n):
                t, g0, count, at = scores_part(n)
                b = t // (NT // B)
                if n == NT:
                    pe.wait_ge(q1_lo_ready, GROUPS)
                wait(pe, max_taken, n - 1)
                for k in range(count):
                    g = g0 + k
                    last = mm(bank[at + k][:, 0:HG * C], q_stack[0:STACK, g, t * P:(t + 1) * P],
                              k_stack[0:STACK, b, g * HG:(g + 1) * HG, :].rearrange("p h c -> p (h c)"),
                              start=True, stop=True)
                last.then_inc(scores_ready, 1)

            def turn_max(t):
                pe.wait_ge(nmax_ready, t + 1)
                nc.tensor.transpose(bank[t // 4][:, (t % 4) * P:(t % 4 + 1) * P], nmax_pad[:, t % 2, :], ident)\
                    .then_inc(nmaxT_psum, 1)

            pe.wait_ge(k_stack_ready, B)
            pe.wait_ge(q_lo_ready, GROUPS)
            for n in range(NT):
                scores(n)
                if n >= 3 and n % 2 == 1:
                    turn_max(n // 2 - 1)
                if n % 2 == 1:
                    queries1(n // 2)
            turn_max(NT // B - 1)

            def values(n):
                b, g = divmod(n, GROUPS)
                pe.wait_ge(exp_done, HG * (n + 1))
                wait(pe, pv_copied, n if n <= GROUPS else n - 1)
                for j in range(HG):
                    last = mm(bank[values_bank(n)][CELL * j:CELL * (j + 1), :], v_ones[:, b, g * HG + j, :],
                              exps[:, (n * HG + j) % NE, :], start=True, stop=True)
                last.then_inc(pv_done, 1)

            def turn_group(n):
                pe.wait_ge(pv_copied, n + 1)
                pe.wait_ge(q_max_ready[0], GROUPS)
                wait(pe, onat_ready, n)
                for t in range(NT // B):
                    last = nc.tensor.transpose(bank[0][:, t * P:(t + 1) * P], pv_sb[:, n % 2, t * P:(t + 1) * P], ident)
                last.then_inc(pv_turned, 1)

            def turn_output(b):
                pe.wait_ge(onat_ready, (b + 1) * GROUPS)
                pe.wait_ge(q_max_ready[1], GROUPS)
                for t in range(NT // B):
                    last = nc.tensor.transpose(bank[1][:, t * P:(t + 1) * P], onat[:, b * (NT // B) + t, :], ident)
                last.then_inc(oT_psum, 1)

            def project(b):
                pe.wait_ge(oT_ready[b], 1)
                for t in range(NT // B):
                    c = slice((b * (NT // B) + t) * P, (b * (NT // B) + t + 1) * P)
                    last = mm(bank[1 - b][:, t * P:(t + 1) * P], oT[:, c], full("wo"), start=True, stop=True)
                last.then_inc(proj_done, 1)

            pe.wait_ge(max_taken, NT)
            for i in range(B * H):
                b, h = divmod(i, H)
                pe.wait_ge(q_max_ready[b], h // HG + 1)
                wait(pe, exp_done, last_in_bank(i) + 1)
                mm(bank[head_bank(i)][0:C, :], k_stack[:, b, h, :], q_stack[:, h // HG, b * T:(b + 1) * T],
                   start=True, stop=True).then_inc(scoresT_ready, 1)
                if i % HG == (HG - 2 if i < H + HG else HG - 1) and i > HG:
                    n = i // HG - 1
                    values(n)
                    if n >= 1:
                        turn_group(n - 1)
                if NAT <= i < NAT + NT:
                    for k in range(2):
                        scores(NT + 2 * (i - NAT) + k)
                if NAT + 3 <= i < NAT + 3 + NT and (i - NAT) % 2 == 1:
                    turn_max(NT // B + (i - NAT - 3) // 2)
                if i == TURN0:
                    turn_output(0)
                if i == TURN0 + 3:
                    project(0)
            values(B * GROUPS - 1)
            turn_group(B * GROUPS - 2)
            turn_group(B * GROUPS - 1)
            turn_output(1)
            project(1)

            pe.wait_ge(eb_lo_ready, 1)
            for k, (t0, t1) in enumerate(GATE_SETS):
                for i, part in enumerate((eb_hi, eb_lo)):
                    mm(bank[2 + k][:, 0:(t1 - t0) * E1].rearrange("p (n e) -> p n e", e=E1), ones_row[:, :],
                       part[:, :].unsqueeze(1).broadcast_to([1, t1 - t0, E1]), start=i == 0, stop=False)
            transpose_rows(3 * NT + B)
            for k, (t0, t1) in enumerate(GATE_SETS):
                for t in range(t0, t1):
                    pe.wait_ge(xT_ready[t // 4], 2)
                    last = mm(bank[2 + k][:, (t - t0) * E1:(t - t0 + 1) * E1], xT[:, t * P:(t + 1) * P], full("rw1"),
                              start=False, stop=t == t1 - 1)
                last.then_inc(logits1, 1)
            for half in range(2):
                mm(acc[half], full("wgs"), xT[:, half * HALF:(half + 1) * HALF], start=True, stop=True)\
                    .then_inc(shared_gate, 1)
            pe.wait_ge(xT_lo_ready, 6)

            def turn_comb1():
                pe.wait_ge(prob_hi_ready, len(GATE_SETS))
                for n, (t0, t1) in enumerate(GATE_SETS):
                    pe.wait_ge(parts1_ready, n + 1)
                    for k in range(KT):
                        for t in range(t0, t1):
                            last = nc.tensor.transpose(bank[2 + k].bitcast(BF16)[:, t * P:(t + 1) * P],
                                                       parts1[:, t, k * ROW_GROUPS:(k + 1) * ROW_GROUPS, :]
                                                       .rearrange("p c r -> p (c r)"), ident_bf[:, :])
                        if n == len(GATE_SETS) - 1:
                            last.then_inc(combT1_psum, 1)

            def combT1_copied():
                pe.wait_ge(combT1_dve, 2)

            def shared_product():
                pe.wait_ge(shared_silu, 2)
                for half in range(2):
                    for t in range(half * NT // 2, (half + 1) * NT // 2):
                        c = slice(t * P, (t + 1) * P)
                        last = mm(acc[half][:, (t % 4) * P:(t % 4 + 1) * P], shared_h[:, c], full("wds"),
                                  start=True, stop=True)
                last.then_inc(shared_down, 1)

            stream(s1, combT1_copied, shared_product, early=turn_comb1)
            transpose_back(1)


def kernel(x, ctx_1024, L0_xattn_conv_w, L0_xattn_conv_b, L0_ffn_router_w, L0_ffn_router_b, L0_ffn_W, L0_ffn_V,
           L0_ffn_W_out, L1_xattn_Wq, L1_xattn_bq, L1_xattn_Wk, L1_xattn_bk, L1_xattn_Wv, L1_xattn_bv, L1_xattn_Wo,
           L1_xattn_bo, L1_ffn_router_w, L1_ffn_expert_bias, L1_ffn_w_gate, L1_ffn_w_down, L1_ffn_w_gate_shared,
           L1_ffn_w_down_shared):
    import numpy as np
    import concourse.bacc as bacc
    from concourse.bass_utils import run_bass_kernel_spmd

    def arr(a):
        return np.asarray(a)

    def stacked(w):
        g = arr(w).T.reshape(P, GROUPS, HG * D)
        return np.concatenate([g, g, g], axis=2).reshape(P, GROUPS * STACK)

    def stacked_bias(v):
        g = arr(v).reshape(GROUPS, HG * D).T
        return np.concatenate([g, g, g], axis=0)

    f32 = np.float32
    ctx = arr(ctx_1024)
    shared_gate = np.concatenate([arr(L1_ffn_w_gate_shared).T, np.zeros((P, P - INTER), f32)], axis=1)
    shared_down = np.concatenate([arr(L1_ffn_w_down_shared).T, np.zeros((P - INTER, P), f32)], axis=0)
    columns = {"rw0": arr(L0_ffn_router_w).T, "ctxT": ctx.reshape(B * C, P).T, "wk": stacked(L1_xattn_Wk),
               "wv": arr(L1_xattn_Wv).T, "wq": stacked(L1_xattn_Wq), "wo": arr(L1_xattn_Wo).T,
               "rw1": arr(L1_ffn_router_w).T, "wgs": shared_gate, "wds": shared_down}
    split_in = np.concatenate([columns[n] for n in SPLIT], axis=1)
    rows_in = np.concatenate([arr(L0_ffn_router_b), arr(L1_xattn_bv), arr(L1_xattn_bo), arr(L1_ffn_expert_bias)])[None, :]
    bqk_in = np.concatenate([stacked_bias(L1_xattn_bq), stacked_bias(L1_xattn_bk)], axis=1)
    w0_in = np.concatenate([arr(L0_ffn_W), arr(L0_ffn_V),
                            arr(L0_ffn_W_out).reshape(E0, HID0 // P, P, P).transpose(0, 2, 1, 3).reshape(E0, P, HID0)],
                           axis=2)
    gate = arr(L1_ffn_w_gate).reshape(KT, ROW_GROUPS, EC // 2, 2, INTER, P).transpose(2, 0, 5, 1, 3, 4)\
        .reshape(ROUNDS1, P, ROW_GROUPS * P)
    down = arr(L1_ffn_w_down).reshape(KT, ROW_GROUPS, EC // 2, 2, P, INTER).transpose(2, 0, 3, 5, 1, 4)\
        .reshape(ROUNDS1, P, ROW_GROUPS * P)
    w1_in = np.concatenate([gate, down], axis=2)

    consts_in = np.zeros((P, NCONST), f32)
    i = np.arange(P)
    consts_in[:, IDENT:IDENT + P] = np.eye(P, dtype=f32)
    consts_in[:, ULT:ULT + P] = i[:, None] < i[None, :]
    consts_in[:, ONES:ONES + P] = 1
    e = np.arange(E0)
    consts_in[:, TRI:TRI + E0 * E0] = (e[None, :] < e[:, None]).reshape(1, E0 * E0)
    for j in range(HG):
        consts_in[:, HMASK + j] = (i % (HG * D)) // D == j
    for h in range(H):
        consts_in[STACK + h, HSEL + h] = 1
        consts_in[STACK + H + h, HSEL + h] = 1
    one = 0x3F80
    sel0_in = np.zeros((E0, 3 * E0, P), np.uint16)
    for n in range(E0):
        sel0_in[n, n::E0, :] = one
    sel1_in = np.zeros((ROUNDS1, P, P), np.uint16)
    for r in range(ROUNDS1):
        for g in range(ROW_GROUPS):
            for part in range(3):
                row = g * CELL + part * EC + 2 * (r // KT)
                sel1_in[r, row, 0:INTER] = one
                sel1_in[r, row + 1, INTER:P] = one

    arrays = {"x": arr(x), "ctx": ctx, "conv_w": arr(L0_xattn_conv_w), "conv_b": arr(L0_xattn_conv_b),
              "split_in": split_in, "consts_in": consts_in, "rows_in": rows_in, "bqk_in": bqk_in, "w0_in": w0_in,
              "sel0_in": sel0_in, "w1_in": w1_in, "sel1_in": sel1_in}
    arrays = {n: np.ascontiguousarray(a) for n, a in arrays.items()}
    nc = bacc.Bacc("TRN2", target_bir_lowering=False, num_devices=1)
    args = [nc.dram_tensor(n, a.shape, mybir.dt.from_np(a.dtype), kind="ExternalInput").ap() for n, a in arrays.items()]
    out = nc.dram_tensor("out", (B, T, P), F32, kind="ExternalOutput").ap()
    build_program(nc, *args, out)
    result = run_bass_kernel_spmd(nc, [arrays], core_ids=[0])
    return result.results[0]["out"]
```
